# Optimizing a Trainium2 kernel written in Bass

```python
import numpy as np
import jax
import jax.numpy as jnp

def _softmax(x, axis=-1):
    return jax.nn.softmax(x, axis=axis)
def _gelu(x):
    return jax.nn.gelu(x, approximate=True)
def _silu(x):
    return jax.nn.silu(x)
def _sigmoid(x):
    return jax.nn.sigmoid(x)
def _layernorm(x, axis=-1, eps=1e-5):
    m = jnp.mean(x, axis=axis, keepdims=True)
    v = jnp.var(x, axis=axis, keepdims=True)
    return (x - m) / jnp.sqrt(v + eps)
def _scatter_add(tgt, idx, src, axis=0):
    return tgt.at[idx].add(src)
def _segment_sum(src, seg, n):
    return jax.ops.segment_sum(src, seg, n)

kernel_name = 'mk_conv_preact_d2_conv_nchw32_f63137'

def setup_inputs(seed: int = 0):
    np.random.seed(seed)
    _w = jnp.asarray
    def _rec_inputs():
        import jax
        import jax.numpy as jnp
        _gk = jax.random.key(seed)
        x = 7.22e-05 + 1 * jax.random.normal(jax.random.fold_in(_gk, 1), (4, 32, 256, 256), jnp.float32)
        return x
    x = _rec_inputs()
    def _L0_conv_setup():
        import jax, jax.numpy as jnp
        import numpy as np
        PI = np.pi
        EPS_A = 0.0001

        def _frft_1d(x, a):
            a = jnp.clip(a, EPS_A, 2.0 - EPS_A)
            N = x.shape[-1]
            x = jnp.fft.ifftshift(x, axes=-1)
            alpha = a * PI / 2.0
            tan_a2 = jnp.tan(a * PI / 4.0)
            sin_a = jnp.sin(alpha)
            n = jnp.arange(N, dtype=jnp.float32) - N // 2
            c1 = jnp.exp(-1j * PI * n ** 2 * tan_a2 / N)
            c2 = jnp.exp(-1j * PI * n ** 2 / (N * sin_a))
            y = jnp.fft.ifft(jnp.fft.fft(x * c1, axis=-1) * c2, axis=-1)
            y = y * c1 / jnp.sqrt(jnp.abs(sin_a) + 1e-12)
            return jnp.fft.fftshift(y, axes=-1)

        def _frft2d(x, ax, ay):
            y = _frft_1d(x, ay)
            y = jnp.swapaxes(_frft_1d(jnp.swapaxes(y, -1, -2), ax), -1, -2)
            return y
        key = jax.random.key(seed)
        kx, = jax.random.split(key, 1)
        B, C, H, W = (4, 32, 256, 256)
        x = jax.random.normal(kx, (B, C, H, W), dtype=jnp.float32)
        alpha = jnp.float32(0.5)
        w = jnp.zeros((C, 2 * C), dtype=jnp.float32)
        w = w.at[jnp.arange(C), jnp.arange(C)].set(1.0)
        return {'x': x, 'alpha': alpha, 'w': w}
    _L0_conv_all = _L0_conv_setup()
    _L0_conv_in = {k: v for k, v in _L0_conv_all.items() if k in ('alpha', 'w', )}
    del _L0_conv_all

    def _L1_conv_setup():
        import jax, jax.numpy as jnp
        import numpy as np
        key = jax.random.key(seed)
        k1, k2 = jax.random.split(key)
        x = jax.random.normal(k1, (8, 32, 252, 252), dtype=jnp.float32)
        weight = jax.random.normal(k2, (32, 32, 5, 5), dtype=jnp.float32)
        return {'x': x, 'weight': weight}
    _L1_conv_all = _L1_conv_setup()
    _L1_conv_in = {k: v for k, v in _L1_conv_all.items() if k in ('weight', )}
    del _L1_conv_all

    return {
        "x": x,
        "L0_conv_alpha": _L0_conv_in["alpha"],
        "L0_conv_w": _L0_conv_in["w"],
        "L1_conv_weight": _L1_conv_in["weight"],
    }

def reference(x, L0_conv_alpha, L0_conv_w, L1_conv_weight):
    import jax
    import jax.numpy as jnp
    def _L0_conv_ref(x, alpha, w):
        import jax, jax.numpy as jnp
        import numpy as np
        PI = np.pi
        EPS_A = 0.0001

        def _frft_1d(x, a):
            a = jnp.clip(a, EPS_A, 2.0 - EPS_A)
            N = x.shape[-1]
            x = jnp.fft.ifftshift(x, axes=-1)
            alpha = a * PI / 2.0
            tan_a2 = jnp.tan(a * PI / 4.0)
            sin_a = jnp.sin(alpha)
            n = jnp.arange(N, dtype=jnp.float32) - N // 2
            c1 = jnp.exp(-1j * PI * n ** 2 * tan_a2 / N)
            c2 = jnp.exp(-1j * PI * n ** 2 / (N * sin_a))
            y = jnp.fft.ifft(jnp.fft.fft(x * c1, axis=-1) * c2, axis=-1)
            y = y * c1 / jnp.sqrt(jnp.abs(sin_a) + 1e-12)
            return jnp.fft.fftshift(y, axes=-1)

        def _frft2d(x, ax, ay):
            y = _frft_1d(x, ay)
            y = jnp.swapaxes(_frft_1d(jnp.swapaxes(y, -1, -2), ax), -1, -2)
            return y
        Xc = x.astype(jnp.complex64)
        Y = _frft2d(Xc, alpha, alpha)
        out = jnp.concatenate([jnp.abs(Y), jnp.angle(Y) / PI], axis=1)
        out = jnp.einsum('oc,bchw->bohw', w, out)
        return out.astype(x.dtype)

    def _L1_conv_ref(x, weight):
        import jax, jax.numpy as jnp
        import numpy as np
        k = weight.shape[-1]
        p = k // 2
        xp = jnp.pad(x, ((0, 0), (0, 0), (p, p), (p, p)), mode='reflect')
        H, W = (xp.shape[-2], xp.shape[-1])
        wp = jnp.zeros((weight.shape[0], weight.shape[1], H, W), dtype=x.dtype)
        wp = wp.at[:, :, :k, :k].set(weight)
        shift = -k // 2
        wp = jnp.roll(wp, shift=(shift, shift), axis=(-2, -1))
        x_fft = jnp.fft.fft2(xp)
        w_fft = jnp.fft.fft2(wp)
        out_fft = jnp.einsum('bihw,oihw->bohw', x_fft, w_fft)
        out = jnp.fft.ifft2(out_fft).real
        return out[:, :, p:-p, p:-p]

    def _gn(v, G=16, eps=1e-5):
        B_, C_, H_, W_ = v.shape
        g = v.reshape(B_, G, C_ // G, H_, W_)
        m = jnp.mean(g, axis=(2, 3, 4), keepdims=True)
        s = jnp.var(g, axis=(2, 3, 4), keepdims=True)
        return ((g - m) / jnp.sqrt(s + eps)).reshape(v.shape)

    def _ln_c(v, eps=1e-6):
        m = jnp.mean(v, axis=1, keepdims=True)
        s = jnp.var(v, axis=1, keepdims=True)
        return (v - m) / jnp.sqrt(s + eps)

    def _ln_t(v, eps=1e-5):
        m = jnp.mean(v, axis=-1, keepdims=True)
        s = jnp.var(v, axis=-1, keepdims=True)
        return (v - m) / jnp.sqrt(s + eps)

    def _to_tokens(v):
        B_, C_, H_, W_ = v.shape
        return v.reshape(B_, C_, H_ * W_).transpose(0, 2, 1)
    def _from_tokens(t, like):
        B_, C_, H_, W_ = like.shape
        return t.transpose(0, 2, 1).reshape(B_, C_, H_, W_)

    x = x + _L0_conv_ref(_gn(x), L0_conv_alpha, L0_conv_w)
    x = x + _L1_conv_ref(_gn(x), L1_conv_weight)
    return x


_drawn_inputs = setup_inputs


def setup_inputs(seed=0):
    import zlib

    import numpy as np

    out = dict(_drawn_inputs(seed))
    spreads = {}
    factors = {}
    for name, (base, spread) in spreads.items():
        noise = np.random.default_rng([zlib.crc32(name.encode()), seed]).standard_normal(out[name].shape)
        drawn = base * np.exp(spread * noise) if base else spread * noise
        out[name] = jnp.asarray(drawn.astype(out[name].dtype))
    for name, factor in factors.items():
        out[name] = (out[name] * factor).astype(out[name].dtype)
    return out
```

```python
from contextlib import ExitStack

import numpy as np

import concourse.bass as bass
from concourse import mybir


P = 128
F32 = mybir.dt.float32
F16 = mybir.dt.float16
I32 = mybir.dt.int32
ALU = mybir.AluOpType
ACT = mybir.ActivationFunctionType
AX_X = mybir.AxisListType.X

PI = float(np.float32(np.pi))
PI_LOW = float(np.pi - np.float64(np.float32(np.pi)))
HALF_PI = float(np.float32(np.pi / 2))
HALF_PI_LOW = float(np.pi / 2 - np.float64(np.float32(np.pi / 2)))
TWO_PI_A = 6.28125
TWO_PI_B = float(np.float32(2 * np.pi - TWO_PI_A))
TWO_PI_C = float(np.float32(2 * np.pi - TWO_PI_A - np.float64(np.float32(2 * np.pi - TWO_PI_A))))
ROUND = 12582912.0
X_SCALE = 64.0
G_SCALE = 4096.0
EPS = 1e-5
SLOTS = 4


def frft_conv_kernel(nc, x, alpha, grid_sq, dft_cos, dft_sin, mix_w, conv_w, tap, quad_mean, out, x1_dram):
    B, C, H, W = x.shape
    Q = P // C
    NPAIR = C // 2
    NB = H // P
    NBLK = H // Q + 1
    NUNIT = NBLK // 2 + 1
    ROWS_Z = H + 4
    WP = W + 4
    KT = 5
    NCHUNK = (NBLK - 1) // 8
    NOUT = H // Q // 2
    PLANE = ROWS_Z * C
    assert P == Q * C and NB == 2 and NBLK == 65 and NUNIT == 33

    with ExitStack() as ctx:
        def sb(name, shape, dt=F32):
            return ctx.enter_context(nc.sbuf_tensor(name, shape, dt))

        def sem(name):
            return ctx.enter_context(nc.semaphore(name))

        psum = ctx.enter_context(nc.psum_tensor("psum", [P, 8, 512], F32))

        arena = sb("arena", [P, 8 * PLANE // 2])
        arena16 = arena[:, :].bitcast(F16)
        Z = arena16.rearrange("p (t k r c) -> p t k r c", t=2, k=4, c=C)
        Zflat = arena16.rearrange("p (l n) -> p l n", l=8)
        conv_in = arena16[:, 0:2 * NBLK * WP].rearrange("p (t j w) -> p t j w", t=2, w=WP)
        dft = arena[:, 0:1024].rearrange("p (s k m) -> p s k m", s=2, k=2)
        kern = arena[:, 1024:3072].rearrange("p (s k n) -> p s k n", s=2, k=2)
        g_tmp = arena[:, 3072:7168].rearrange("p (i m) -> p i m", m=256)
        g_full = arena[:, 7168:8192].rearrange("p (j n) -> p j n", j=2)

        G = sb("G", [P, 2, NB, 768], F16)
        mixw = sb("mixw", [P, 2, P])
        convw = sb("convw", [P, 2, 2, KT, P], F16)
        tapm = sb("tapm", [P, 2, P])
        quadm = sb("quadm", [P, P])
        ones = sb("ones", [P, P])
        raw = sb("raw", [P, 2, 2, NB, W])
        split = sb("split", [P, 2, 2, 2, NB, W], F16)
        res = sb("res", [P, SLOTS, 2, W])
        work = sb("work", [P, 8192])
        sq = work[:, 0:4096].rearrange("p (s k j w) -> p s k j w", s=SLOTS, k=2, j=2)
        mag = work[:, 4096:6144].rearrange("p (s j w) -> p s j w", s=SLOTS, j=2)
        ang = work[:, 6144:8192].rearrange("p (s j w) -> p s j w", s=SLOTS, j=2)
        x1t = work[:, 0:2 * 8 * WP].rearrange("p (s j w) -> p s j w", s=2, w=WP)
        convw_raw = work[:, 4160:4160 + 2 * KT * P].rearrange("p (k t n) -> p k t n", k=2, t=KT)
        stat_in = work[:, 5440:7488].rearrange("p (s c n) -> p s c n", s=2, c=2)

        grid = sb("grid", [P, 2, 260])
        ang_s = sb("ang_s", [P, 3, 3])
        sc = sb("sc", [P, 16])
        bst1 = sb("bst1", [P, C, 6])
        mv1 = sb("mv1", [P, NPAIR, 2])
        gn1 = sb("gn1", [P, 6, NPAIR])
        bst2 = sb("bst2", [P, NBLK, 6])
        gn2 = sb("gn2", [P, 16])
        wmax = sb("wmax", [P, 3])
        tiny = sb("tiny", [P, 1])

        names = """consts_in setup_v setup_a setup_p g_ready raw_in0 raw_in1 raw_n raw_hi raw_lo s1_mm s1_free z_hi z_lo z_pad
            s2_mm s2_free sq_done sum_done r_done d_done rec_done u_done at_done ang_done mix_mm x1_done
            st2_done res_in0 res_in1 res_in2 res_in3 x1_out0 x1_out1 x1_out2 x1_out3
            st_in0 st_in1 st1_done st1_v st1_p st1_a sc1_ready gn2_v gn2_p gn2_a w_in w_ready
            xc_in0 xc_in1 xc_pad xc_n xc_hi xc_lo cv_mm cv_free cv_out0 cv_out1 cv_out2 cv_out3 sgn_done
            setup_p_mm link1 link2""".split()
        S = {n: sem(n) for n in names}
        raw_in = [S["raw_in0"], S["raw_in1"]]
        res_in = [S[f"res_in{i}"] for i in range(SLOTS)]
        x1_out = [S[f"x1_out{i}"] for i in range(SLOTS)]
        st_in = [S["st_in0"], S["st_in1"]]
        xc_in = [S["xc_in0"], S["xc_in1"]]
        cv_out = [S[f"cv_out{i}"] for i in range(SLOTS)]

        x_rows = x.rearrange("b c (k p) w -> b p c k w", p=P)
        x_stat = x.rearrange("b c (p r) w -> b p c (r w)", p=P)

        def slot(s):
            return psum[:, 2 * s:2 * s + 2, :]

        def slot_re(s, n):
            return psum[:, 2 * s:2 * s + n, 0:256]

        def slot_im(s, n):
            return psum[:, 2 * s:2 * s + n, 256:512]

        def slot_mix(s, n):
            return psum[:, 2 * s, 0:256 * n].rearrange("p (j w) -> p j w", j=n)

        def walk(eng, step, drains):
            step(0, 0, 2)
            step(1, 1, 2)
            with eng.Fori(0, 7) as i:
                for q in range(4):
                    step(4 * i + (q + 2), (q + 2) % 4, 2)
            step(30, 2, 2)
            step(31, 3, 2)
            step(32, 0, 1)
            for u in range(33, 33 + drains):
                step(u, u % 4, 0)

        def blocks_of(u):
            return 1 if isinstance(u, int) and u == NUNIT - 1 else 2

        def batches(eng, body):
            with eng.Fori(0, B - 1) as b:
                body(b, True)
            body(B - 1, False)

        block = ctx.enter_context(nc.Block())

        @block.sync
        def _(sp):
            sp.dma_start(grid[:, 0, :], grid_sq).then_inc(S["consts_in"], 16)
            sp.dma_start(sc[:, 0:1], alpha.to_broadcast([P, 1])).then_inc(S["consts_in"], 16)
            sp.dma_start(dft[:, 0, :, :], dft_cos.rearrange("(k p) m -> p k m", p=P)).then_inc(S["consts_in"], 16)
            sp.dma_start(dft[:, 1, :, :], dft_sin.rearrange("(k p) m -> p k m", p=P)).then_inc(S["consts_in"], 16)
            sp.dma_start(mixw[:, :, :], mix_w).then_inc(S["consts_in"], 16)
            sp.dma_start(tapm[:, :, :], tap).then_inc(S["consts_in"], 16)
            sp.dma_start(quadm[:, :], quad_mean).then_inc(S["consts_in"], 16)

            def load_res(b, u, s, n):
                for q in range(Q):
                    if isinstance(u, int) and u == 0 and q == 0:
                        rows = x[bass.ds(b, 1), :, 1:4:2, :]
                    elif n == 1:
                        r = [H - 1, H - 2, H - 3, 2][q]
                        rows = x[bass.ds(b, 1), :, r:r + 1, :]
                    else:
                        rows = x[bass.ds(b, 1), :, bass.ds(8 * u + (q - 1), 2, step=4), :]
                    sp.dma_start(res[C * q:C * q + C, s, 0:n, :], rows.rearrange("b c r w -> (b c) r w"))\
                      .then_inc(res_in[s], 16)

            def body(b, more):
                with sp.Fori(0, NPAIR // 2) as i:
                    for k in range(2):
                        sp.wait_ge(S["raw_lo"], b * NPAIR + 2 * i + (k + 1))
                        sp.dma_start(raw[:, k, :, :, :], x_rows[bass.ds(b, 1), :, bass.ds(4 * i + 2 * k, 2), :, :]
                                     .rearrange("b p c k w -> (b p) c k w")).then_inc(raw_in[k], 16)

                for s in range(SLOTS):
                    sp.wait_ge(cv_out[s], b * (NOUT // SLOTS) * 64 + 64)
                for u in range(3):
                    load_res(b, u, u, 2)

                def step(u, s, n):
                    if n:
                        sp.wait_ge(S["x1_done"], b * NUNIT + u + 1)
                        sp.dma_start(x1_dram[bass.ds(b, 1), :, bass.ds(2 * u, n), :].rearrange("b p j w -> (b p) j w"),
                                     res[:, s, 0:n, :]).then_inc(x1_out[s], 16)
                    nu = u + 3
                    if not isinstance(u, int) or nu < NUNIT:
                        if not isinstance(u, int) or nu >= SLOTS:
                            ns = (s + 3) % 4
                            per = 9 if ns == 0 else 8
                            if isinstance(u, int):
                                sp.wait_ge(x1_out[ns], b * (16 * per) + 16 * ((nu - ns) // 4))
                            else:
                                sp.wait_ge(x1_out[ns], b * (16 * per) + 4 * (nu - ns))
                        load_res(b, nu, (s + 3) % 4, 1 if isinstance(nu, int) and nu == NUNIT - 1 else 2)

                step(0, 0, 2)
                step(1, 1, 2)
                with sp.Fori(0, 6) as i:
                    for q in range(4):
                        step(4 * i + (q + 2), (q + 2) % 4, 2)
                for u in range(26, NUNIT):
                    step(u, u % 4, 2 if u < NUNIT - 1 else 1)

                for s in (1, 2, 3):
                    sp.wait_ge(x1_out[s], (b + 1) * (16 * 8))
                sp.dma_start(convw_raw, conv_w).then_inc(S["w_in"], 16)
                sp.wait_ge(x1_out[0], (b + 1) * (16 * 9))

                def load_x1(c, s, n):
                    sp.dma_start(x1t[:, s, 0:n, 1:1 + W], x1_dram[bass.ds(b, 1), :, bass.ds(8 * c, n), :]
                                 .rearrange("b p j w -> (b p) j w")).then_inc(xc_in[s], 16)

                load_x1(0, 0, 8)
                load_x1(1, 1, 8)

                def store_out(c, k):
                    sp.wait_ge(S["cv_free"], b * NOUT + 4 * c + (k + 1 + SLOTS))
                    for q in range(Q):
                        sp.dma_start(out[bass.ds(b, 1), :, bass.ds(32 * c + (8 * k + q), 2, step=4), :]
                                     .rearrange("b c r w -> (b c) r w"), res[C * q:C * q + C, k, :, :])\
                          .then_inc(cv_out[k], 16)

                def chunk(c, s, n):
                    if n:
                        sp.wait_ge(S["xc_lo"], b * (NCHUNK + 1) + c + 1)
                        sp.wait_ge(S["xc_hi"], b * (NCHUNK + 1) + c + 1)
                        load_x1(c + 2, s, n)
                    for k in range(4):
                        store_out(c, k)

                with sp.Fori(0, 3) as i:
                    for k in range(2):
                        chunk(2 * i + k, k, 8)
                chunk(6, 0, 1)
                chunk(7, 1, 0)

            batches(sp, body)
            for s in range(SLOTS):
                sp.wait_ge(cv_out[s], B * (NOUT // SLOTS) * 64 + 64)

        @block.gpsimd
        def _(pool):
            pool.sem_inc(S["raw_lo"], 2)
            pool.sem_inc(S["s1_free"], SLOTS)
            pool.sem_inc(S["s2_free"], SLOTS)
            pool.sem_inc(S["cv_free"], SLOTS)
            for s in range(SLOTS):
                pool.sem_inc(cv_out[s], 64)

            def load_stat_at(b, g, k, first=False):
                if not first:
                    pool.wait_ge(S["st1_done"], b * C + 2 * g - 2)
                pool.dma_start(stat_in[:, k, :, :], x_stat[bass.ds(b, 1), :, bass.ds(2 * g, 2), :]
                               .rearrange("b p c n -> (b p) c n")).then_inc(st_in[k], 16)

            for g in range(NPAIR):
                load_stat_at(0, g, g % 2, first=g < 2)

            def body(b, more):
                with pool.Fori(0, NPAIR // 2) as i:
                    for k in range(2):
                        g = 2 * i + k
                        pool.wait_ge(S["raw_hi"], b * NPAIR + g + 1)
                        nc.gpsimd.tensor_tensor(split[:, k, 1], raw[:, k], split[:, k, 0], ALU.subtract)\
                            .then_inc(S["raw_lo"], 1)

                def step(u, s, n):
                    pool.wait_ge(S["sq_done"], b * NUNIT + u + 1)
                    nc.gpsimd.tensor_tensor(sq[:, s, 0, 0:n], sq[:, s, 0, 0:n], sq[:, s, 1, 0:n], ALU.add)\
                        .then_inc(S["sum_done"], 1)
                    pool.wait_ge(S["r_done"], b * NUNIT + u + 1)
                    nc.gpsimd.tensor_tensor(sq[:, s, 0, 0:n], sq[:, s, 1, 0:n], mag[:, s, 0:n], ALU.add)\
                        .then_inc(S["d_done"], 1)

                walk(pool, step, 0)

                pool.wait_ge(S["x1_done"], (b + 1) * NUNIT)

                def chunk(c, s, n):
                    if more:
                        for k in range(2):
                            if isinstance(c, int) and c == 0:
                                load_stat_at(b + 1, 0 + k, k, first=True)
                            else:
                                load_stat_at(b + 1, 2 * c + k, k)
                    pool.wait_ge(S["xc_hi"], b * (NCHUNK + 1) + c + 1)
                    j = 8 * c
                    nc.gpsimd.tensor_tensor(conv_in[:, 1, bass.ds(j, n), :], x1t[:, s, 0:n, :],
                                            conv_in[:, 0, bass.ds(j, n), :], ALU.subtract).then_inc(S["xc_lo"], 1)

                chunk(0, 0, 8)
                chunk(1, 1, 8)
                with pool.Fori(1, 4) as i:
                    for k in range(2):
                        chunk(2 * i + k, k, 8)
                pool.wait_ge(S["xc_hi"], b * (NCHUNK + 1) + NCHUNK + 1)
                nc.gpsimd.tensor_tensor(conv_in[:, 1, NBLK - 1, :], x1t[:, 0, 0, :], conv_in[:, 0, NBLK - 1, :],
                                        ALU.subtract).then_inc(S["xc_lo"], 1)

            batches(pool, body)

        @block.scalar
        def _(act):
            act.wait_ge(S["setup_v"], 1)
            nc.scalar.activation(grid[:, 0, :], grid[:, 1, :], ACT.Sin).then_inc(S["setup_a"], 1)
            act.wait_ge(S["setup_v"], 2)
            nc.scalar.activation(grid[:, 1, :], grid[:, 1, :], ACT.Sin).then_inc(S["setup_a"], 1)

            def root_of_variance1(b):
                act.wait_ge(S["st1_v"], b * 3 + 3)
                nc.scalar.activation(gn1[:, 3, :], gn1[:, 1, :], ACT.Sqrt).then_inc(S["st1_a"], 1)

            root_of_variance1(0)

            def body(b, more):
                def pair_hi(g, k):
                    act.wait_ge(S["raw_n"], b * NPAIR + g + 1)
                    nc.scalar.copy(split[:, k, 0], raw[:, k]).then_inc(S["raw_hi"], 1)

                pair_hi(0, 0)
                pair_hi(1, 1)
                with act.Fori(0, NPAIR // 2 - 1) as i:
                    for k in range(2):
                        for e in range(2):
                            product_hi_at(act, b, i, k, e)
                        pair_hi(2 * i + (k + 2), k)
                for k in range(2):
                    for e in range(2):
                        product_hi_at(act, b, NPAIR // 2 - 1, k, e)

                def step(u, s, n):
                    if n:
                        act.wait_ge(S["s2_mm"], b * NUNIT + u + 1)
                        act.wait_ge(S["s2_free"], b * NUNIT + u + 1)
                        nc.scalar.activation(sq[:, s, 0, 0:n], slot_re(s, n), ACT.Square)
                        nc.scalar.activation(sq[:, s, 1, 0:n], slot_im(s, n), ACT.Square).then_inc(S["sq_done"], 1)
                        act.wait_ge(S["sum_done"], b * NUNIT + u + 1)
                        nc.scalar.activation(mag[:, s, 0:n], sq[:, s, 0, 0:n], ACT.Sqrt, bias=tiny[:, 0:1])
                        nc.scalar.activation(sq[:, s, 1, 0:n], slot_im(s, n), ACT.Abs).then_inc(S["r_done"], 1)
                    if not isinstance(u, int) or u >= 1:
                        v, t, m = u - 1, (s + 3) % 4, blocks_of(u - 1)
                        act.wait_ge(S["u_done"], b * NUNIT + v + 1)
                        nc.scalar.activation(ang[:, t, 0:m], ang[:, t, 0:m], ACT.Arctan).then_inc(S["at_done"], 1)
                        nc.scalar.activation(sq[:, t, 1, 0:m], sgn_in(t, m), ACT.Sign).then_inc(S["sgn_done"], 1)

                walk(act, step, 1)

                act.wait_ge(S["gn2_v"], b * 4 + 3)
                nc.scalar.activation(gn2[:, 5:6], gn2[:, 4:5], ACT.Sqrt).then_inc(S["gn2_a"], 1)

                def chunk_hi(c, s, n):
                    act.wait_ge(S["xc_n"], b * (NCHUNK + 1) + c + 1)
                    nc.scalar.copy(conv_in[:, 0, bass.ds(8 * c, n), :], x1t[:, s, 0:n, :]).then_inc(S["xc_hi"], 1)

                def rows_out(c, k):
                    act.wait_ge(S["cv_mm"], b * NOUT + 4 * c + (k + 1))
                    act.wait_ge(cv_out[k], (b * (NOUT // SLOTS) + c) * 64 + 64)
                    nc.scalar.activation(res[:, k, :, :], psum[:, k, :].rearrange("p (j w) -> p j w", j=2),
                                         ACT.Identity, bias=gn2[:, 8:9], scale=gn2[:, 9:10])\
                        .then_inc(S["cv_free"], 1)

                chunk_hi(0, 0, 8)

                def chunk(c, s, n):
                    chunk_hi(c + 1, 1 - s, n)
                    for k in range(4):
                        rows_out(c, k)

                with act.Fori(0, 3) as i:
                    for k in range(2):
                        chunk(2 * i + k, k, 8)
                chunk(6, 0, 8)
                chunk(7, 1, 1)
                if more:
                    root_of_variance1(b + 1)

            def product_hi_at(act, b, i, k, e):
                c = 4 * i + (2 * k + e)
                s = 2 * k + e
                act.wait_ge(S["s1_mm"], b * C + c + 1)
                nc.scalar.activation(Z[:, 0, :, 1:1 + H, bass.ds(c, 1)].rearrange("p k r c -> p k (r c)"),
                                     slot(s).rearrange("p j (k r) -> p (j k) r", k=2),
                                     ACT.Copy, scale=1.0 / G_SCALE).then_inc(S["z_hi"], 1)

            def sgn_in(t, m):
                return slot_im(t, m)

            batches(act, body)

        @block.vector
        def _(dve):
            V = nc.vector
            chain = [0]
            link_sem = S["setup_p"]

            def link(ins):
                chain[0] += 1
                ins.then_inc(link_sem, 1)
                dve.wait_ge(link_sem, chain[0])

            V.memset(ones[:, :], 1.0 / P)
            V.memset(tiny[:, :], 2.0 ** -60)
            dve.wait_ge(S["consts_in"], 16 * 7)
            a = sc[:, 1:2]
            link(V.tensor_scalar(a, sc[:, 0:1], float(np.float32(1e-4)), float(np.float32(2.0 - 1e-4)), ALU.max, ALU.min))
            y, z, acc = ang_s[:, 0, :], ang_s[:, 1, :], ang_s[:, 2, :]
            link(V.tensor_scalar(sc[:, 2:3], a, PI, None, ALU.mult))
            link(V.tensor_scalar(y[:, 0:1], sc[:, 2:3], 0.5, None, ALU.mult))
            link(V.tensor_scalar(y[:, 1:2], sc[:, 2:3], 0.25, None, ALU.mult))
            link(V.tensor_scalar(y[:, 2:3], y[:, 1:2], -1.0, HALF_PI, ALU.mult, ALU.add))
            link(V.tensor_scalar(y[:, 2:3], y[:, 2:3], HALF_PI_LOW, None, ALU.add))
            link(V.tensor_scalar(sc[:, 3:4], y[:, 0:1], -1.0, PI, ALU.mult, ALU.add))
            link(V.tensor_scalar(sc[:, 3:4], sc[:, 3:4], PI_LOW, None, ALU.add))
            link(V.tensor_tensor(y[:, 0:1], y[:, 0:1], sc[:, 3:4], ALU.min))
            link(V.tensor_tensor(z, y, y, ALU.mult))
            fact = [-1 / 6, 1 / 120, -1 / 5040, 1 / 362880, -1 / 39916800, 1 / 6227020800, -1 / 1307674368000]
            link(V.tensor_scalar(acc, z, fact[6], fact[5], ALU.mult, ALU.add))
            for f in fact[4::-1]:
                link(V.tensor_tensor(acc, acc, z, ALU.mult))
                link(V.tensor_scalar(acc, acc, f, None, ALU.add))
            link(V.tensor_tensor(acc, acc, z, ALU.mult))
            link(V.tensor_tensor(acc, acc, y, ALU.mult))
            link(V.tensor_tensor(acc, acc, y, ALU.add))
            link(V.reciprocal(sc[:, 4:5], acc[:, 2:3]))
            link(V.tensor_tensor(sc[:, 5:6], acc[:, 1:2], sc[:, 4:5], ALU.mult))
            link(V.tensor_scalar(sc[:, 6:7], acc[:, 0:1], float(W), None, ALU.mult))
            link(V.reciprocal(sc[:, 7:8], sc[:, 6:7]))
            link(V.tensor_scalar(sc[:, 8:9], acc[:, 0:1], 1e-12, None, ALU.add))
            link(V.reciprocal(sc[:, 9:10], sc[:, 8:9]))
            link(V.tensor_scalar(mixw[:, 0, :], mixw[:, 0, :], sc[:, 9:10], 1.0 / (X_SCALE * G_SCALE), ALU.mult, ALU.mult))
            link(V.tensor_scalar(mixw[:, 1, :], mixw[:, 1, :], -2.0 / float(np.pi), None, ALU.mult))
            th, kk = grid[:, 0, :], grid[:, 1, :]
            link(V.tensor_scalar(th, th, PI, None, ALU.mult))
            link(V.tensor_scalar(th[:, 0:2], th[:, 0:2], sc[:, 5:6], 1.0 / W, ALU.mult, ALU.mult))
            link(V.tensor_scalar(th[:, 4:260], th[:, 4:260], sc[:, 5:6], 1.0 / W, ALU.mult, ALU.mult))
            link(V.tensor_scalar(th[:, 2:4], th[:, 2:4], sc[:, 7:8], None, ALU.mult))
            link(V.tensor_scalar(kk, th, float(1 / (2 * np.pi)), ROUND, ALU.mult, ALU.add))
            link(V.tensor_scalar(kk, kk, ROUND, None, ALU.subtract))
            for part in (TWO_PI_A, TWO_PI_B, TWO_PI_C):
                link(V.scalar_tensor_tensor(th, kk, -part, th, ALU.mult, ALU.add))
            V.tensor_scalar(kk, th, 3.1415925, -3.1415925, ALU.min, ALU.max).then_inc(S["setup_v"], 1)
            dve.wait_ge(S["setup_a"], 1)
            dve.wait_ge(S["setup_v"], 1)
            link(V.scalar_tensor_tensor(kk, kk, -1.0, kk, ALU.mult, ALU.max))
            V.tensor_scalar(kk, kk, -1.0, HALF_PI, ALU.mult, ALU.add).then_inc(S["setup_v"], 1)
            dve.wait_ge(S["setup_a"], 2)
            sin_, cos_ = th, kk
            link(V.tensor_scalar(sc[:, 10:12], sin_[:, 2:4], -1.0, None, ALU.mult))
            for t in range(2):
                for k in range(2):
                    V.tensor_scalar(kern[:, t, k, 0:256], dft[:, t, k, :], cos_[:, 2 + k:3 + k], None, ALU.mult)
                    ins = V.tensor_scalar(kern[:, t, k, 256:512], dft[:, t, k, :], sc[:, 10 + k:11 + k], None, ALU.mult)
            ins.then_inc(S["g_ready"], 1)
            link(V.tensor_scalar(sc[:, 12:14], cos_[:, 0:2], G_SCALE / W, None, ALU.mult))
            link(V.tensor_scalar(sc[:, 14:16], sin_[:, 0:2], G_SCALE / W, None, ALU.mult))
            dve.wait_ge(S["setup_p_mm"], 1)
            for j in range(2):
                cr, ci = psum[:, j, 0:256], psum[:, j, 256:512]
                cp, sp_ = sc[:, 12 + j:13 + j], sc[:, 14 + j:15 + j]
                t0, t1, ur, ui = (g_tmp[:, 4 * j + n, :] for n in range(4))
                rc, rs = cos_[:, 4:260], sin_[:, 4:260]
                link(V.tensor_scalar(t0, cr, cp, None, ALU.mult))
                link(V.scalar_tensor_tensor(ur, ci, sp_, t0, ALU.mult, ALU.add))
                link(V.tensor_scalar(t1, cr, sp_, None, ALU.mult))
                link(V.scalar_tensor_tensor(ui, ci, cp, t1, ALU.mult, ALU.subtract))
                gr, gi = g_full[:, j, 0:256], g_full[:, j, 256:512]
                link(V.tensor_tensor(t0, ur, rc, ALU.mult))
                link(V.tensor_tensor(t1, ui, rs, ALU.mult))
                link(V.tensor_tensor(gr, t0, t1, ALU.add))
                link(V.tensor_tensor(t0, ui, rc, ALU.mult))
                link(V.tensor_tensor(t1, ur, rs, ALU.mult))
                link(V.tensor_tensor(gi, t0, t1, ALU.subtract))
                link(V.tensor_copy(G[:, 0, j, 256:768], g_full[:, j, :]))
                link(V.tensor_tensor(G[:, 1, j, 256:768], g_full[:, j, :], G[:, 0, j, 256:768], ALU.subtract))
                for t in range(2):
                    link(V.tensor_scalar(G[:, t, j, 0:256], G[:, t, j, 512:768], -1.0, None, ALU.mult))
            V.memset(sc[:, 0:1], 0.0).then_inc(S["g_ready"], 1)

            def pair_stats(b, g, k):
                dve.wait_ge(st_in[k], b * (8 * NPAIR) + g * 8 + 16 - 8 * k)
                for e in range(2):
                    V.bn_stats(bst1[:, bass.ds(2 * g + e, 1), :].rearrange("p c s -> p (c s)"), stat_in[:, k, e, :])\
                        .then_inc(S["st1_done"], 1)

            def finish_stats1(b):
                dve.wait_ge(S["st1_done"], (b + 1) * C)
                V.memset(gn1[:, 2:4, :], 0.0)
                for g in range(NPAIR):
                    ins = V.bn_aggr(mv1[:, g, :], bst1[:, 2 * g:2 * g + 2, :].rearrange("p c s -> p (c s)"))
                ins.then_inc(S["st1_v"], 1)
                mean, var, w0, w1 = (gn1[:, n, :] for n in range(4))
                dve.wait_ge(S["st1_p"], b * 2 + 1)
                lk = link1
                lk(V.tensor_copy(gn1[:, 0:2, :], psum[:, 6, 0:2 * NPAIR].rearrange("p (g s) -> p s g", s=2)), b, 1)
                lk(V.tensor_tensor(w0, mv1[:, :, 0], mean, ALU.subtract), b, 2)
                V.tensor_tensor(w0, w0, w0, ALU.mult).then_inc(S["st1_v"], 1)
                dve.wait_ge(S["st1_p"], b * 2 + 2)
                dve.wait_ge(S["st1_v"], b * 3 + 2)
                V.scalar_tensor_tensor(var, psum[:, 6, 64:64 + NPAIR], EPS, var, ALU.add, ALU.add)\
                    .then_inc(S["st1_v"], 1)
                dve.wait_ge(S["st1_a"], b + 1)
                dve.wait_ge(S["st1_v"], b * 3 + 3)
                lk(V.reciprocal(w0, w1), b, 3)
                lk(V.tensor_tensor(w0, w0, var, ALU.mult), b, 4)
                lk(V.tensor_tensor(w0, w0, w1, ALU.add), b, 5)
                lk(V.tensor_scalar(w0, w0, 0.5, None, ALU.mult), b, 6)
                lk(V.reciprocal(w0, w0), b, 7)
                lk(V.tensor_scalar(gn1[:, 4, :], w0, X_SCALE, None, ALU.mult), b, 8)
                lk(V.tensor_tensor(w0, mean, gn1[:, 4, :], ALU.mult), b, 9)
                lk(V.tensor_scalar(gn1[:, 5, :], w0, -1.0, None, ALU.mult), b, 10)

            LINKS1 = 10

            def link1(ins, b, n):
                ins.then_inc(S["link1"], 1)
                dve.wait_ge(S["link1"], b * LINKS1 + n)

            with dve.Fori(0, NPAIR // 2) as i:
                for k in range(2):
                    pair_stats(0, 2 * i + k, k)
            finish_stats1(0)

            LINKS2 = 16

            def link2(ins, b, n):
                ins.then_inc(S["link2"], 1)
                dve.wait_ge(S["link2"], b * LINKS2 + n)

            def body(b, more):
                def normalise(g, k):
                    dve.wait_ge(raw_in[k], b * (8 * NPAIR) + g * 8 + 16 - 8 * k)
                    V.tensor_scalar(raw[:, k], raw[:, k], gn1[:, 4, bass.ds(g, 1)], gn1[:, 5, bass.ds(g, 1)],
                                    ALU.mult, ALU.add).then_inc(S["raw_n"], 1)

                def product_lo(c, s):
                    dve.wait_ge(S["z_hi"], b * C + c + 1)
                    V.scalar_tensor_tensor(Z[:, 1, :, 1:1 + H, bass.ds(c, 1)].rearrange("p k r c -> p k (r c)"),
                                           slot(s).rearrange("p j (k r) -> p (j k) r", k=2), 1.0 / G_SCALE,
                                           Z[:, 0, :, 1:1 + H, bass.ds(c, 1)].rearrange("p k r c -> p k (r c)"),
                                           ALU.mult, ALU.subtract).then_inc(S["s1_free"], 1)

                normalise(0, 0)
                normalise(1, 1)
                with dve.Fori(0, NPAIR // 2 - 1) as i:
                    for k in range(2):
                        for e in range(2):
                            product_lo(4 * i + (2 * k + e), 2 * k + e)
                        normalise(2 * i + (k + 2), k)
                for k in range(2):
                    for e in range(2):
                        product_lo(C - 4 + 2 * k + e, 2 * k + e)
                dve.wait_ge(S["s1_free"], (b + 1) * C + SLOTS)
                for n, (to, of) in enumerate(((0, 2), (H + 1, H - 1), (H + 2, H - 2), (H + 3, 3))):
                    V.tensor_copy(Zflat[:, :, to * C:to * C + C], Zflat[:, :, of * C:of * C + C])\
                        .then_inc(S["z_pad"], 1)

                def step(u, s, n):
                    if n:
                        d = sq[:, s, 0, 0:n]
                        dve.wait_ge(S["d_done"], b * NUNIT + u + 1)
                        V.reciprocal(d, d).then_inc(S["rec_done"], 1)
                        dve.wait_ge(S["rec_done"], b * NUNIT + u + 1)
                        V.tensor_tensor(ang[:, s, 0:n], slot_re(s, n), d, ALU.mult).then_inc(S["u_done"], 1)
                    if not isinstance(u, int) or 1 <= u <= NUNIT:
                        v, t, m = u - 1, (s + 3) % 4, blocks_of(u - 1)
                        dve.wait_ge(S["sgn_done"], b * NUNIT + v + 1)
                        V.scalar_tensor_tensor(ang[:, t, 0:m], ang[:, t, 0:m], float(np.pi / 4), sq[:, t, 1, 0:m],
                                               ALU.subtract, ALU.mult).then_inc(S["ang_done"], 1)
                    if not isinstance(u, int) or u >= 2:
                        v, t, m = u - 2, (s + 2) % 4, blocks_of(u - 2)
                        per = 9 if t == 0 else 8
                        dve.wait_ge(S["mix_mm"], b * NUNIT + v + 1)
                        if isinstance(v, int):
                            dve.wait_ge(res_in[t], b * (64 * per) + 64 * (v // 4 + 1))
                        else:
                            dve.wait_ge(res_in[t], b * (64 * per) + 16 * v + (64 - 16 * t))
                        V.tensor_tensor(res[:, t, 0:m, :], slot_mix(t, m), res[:, t, 0:m, :], ALU.add)\
                            .then_inc(S["x1_done"], 1)
                        dve.wait_ge(S["x1_done"], b * NUNIT + v + 1)
                        for e in range(m):
                            V.bn_stats(bst2[:, bass.ds(2 * v + e, 1), :].rearrange("p c s -> p (c s)"),
                                       res[:, t, e, :]).then_inc(S["s2_free"] if e == m - 1 else S["st2_done"], 1)

                walk(dve, step, 2)

                dve.wait_ge(S["s2_free"], (b + 1) * NUNIT + SLOTS)
                dve.wait_ge(S["st2_done"], (b + 1) * (NUNIT - 1))
                lk = link2
                lk(V.tensor_copy(bst2[0:C, 0, :], bst2[0:C, NBLK - 1, :]), b, 1)
                V.memset(wmax[:, :], 0.0)
                V.bn_aggr(gn2[:, 0:2], bst2[:, 0:NBLK - 1, :].rearrange("p j s -> p (j s)")).then_inc(S["gn2_v"], 1)
                dve.wait_ge(S["gn2_p"], b * 3 + 1)
                lk(V.tensor_copy(gn2[:, 2:4], psum[:, 7, 0:2]), b, 2)
                lk(V.tensor_tensor(gn2[:, 6:7], gn2[:, 0:1], gn2[:, 2:3], ALU.subtract), b, 3)
                V.tensor_tensor(gn2[:, 7:8], gn2[:, 6:7], gn2[:, 6:7], ALU.mult).then_inc(S["gn2_v"], 1)
                dve.wait_ge(S["gn2_p"], b * 3 + 2)
                dve.wait_ge(S["gn2_v"], b * 4 + 2)
                V.scalar_tensor_tensor(gn2[:, 4:5], psum[:, 7, 2:3], EPS, gn2[:, 3:4], ALU.add, ALU.add)\
                    .then_inc(S["gn2_v"], 1)
                dve.wait_ge(S["gn2_a"], b + 1)
                dve.wait_ge(S["gn2_v"], b * 4 + 3)
                lk(V.reciprocal(gn2[:, 6:7], gn2[:, 5:6]), b, 4)
                lk(V.tensor_tensor(gn2[:, 6:7], gn2[:, 6:7], gn2[:, 4:5], ALU.mult), b, 5)
                lk(V.tensor_tensor(gn2[:, 6:7], gn2[:, 6:7], gn2[:, 5:6], ALU.add), b, 6)
                lk(V.tensor_scalar(gn2[:, 10:11], gn2[:, 6:7], 0.5, None, ALU.mult), b, 7)
                lk(V.reciprocal(gn2[:, 7:8], gn2[:, 10:11]), b, 8)
                lk(V.tensor_scalar(gn2[:, 11:12], gn2[:, 7:8], X_SCALE, None, ALU.mult), b, 9)
                lk(V.scalar_tensor_tensor(gn2[:, 12:13], gn2[:, 2:3], -1.0, gn2[:, 11:12], ALU.mult, ALU.mult), b, 10)
                dve.wait_ge(S["w_in"], (b + 1) * 16)
                V.tensor_reduce(wmax[:, 2:3], convw_raw, mybir.AxisListType.XYZ, ALU.min)
                lk(V.tensor_reduce(wmax[:, 0:1], convw_raw, mybir.AxisListType.XYZ, ALU.max), b, 11)
                lk(V.scalar_tensor_tensor(wmax[:, 0:1], wmax[:, 2:3], -1.0, wmax[:, 0:1], ALU.mult, ALU.max), b, 12)
                V.tensor_tensor(wmax[:, 1:2], wmax[:, 0:1], gn2[:, 10:11], ALU.add).then_inc(S["gn2_v"], 1)
                lk(V.scalar_tensor_tensor(convw_raw[:, :, 3, :], tapm[:, :, :], gn2[:, 10:11], convw_raw[:, :, 3, :],
                                          ALU.mult, ALU.add), b, 13)
                dve.wait_ge(S["gn2_p"], b * 3 + 3)
                lk(V.tensor_scalar(gn2[:, 13:14].bitcast(I32), psum[:, 7, 3:4].bitcast(I32), 0x7F800000, None,
                                   ALU.bitwise_and), b, 14)
                lk(V.tensor_scalar(gn2[:, 9:10], gn2[:, 13:14], 2.0 ** -14 / X_SCALE, None, ALU.mult), b, 15)
                lk(V.reciprocal(gn2[:, 14:15], gn2[:, 13:14]), b, 16)
                V.tensor_copy(gn2[:, 8:9], gn2[:, 2:3])
                V.tensor_scalar(convw_raw, convw_raw, gn2[:, 14:15], 2.0 ** 14, ALU.mult, ALU.mult)\
                    .then_inc(S["w_ready"], 1)
                dve.wait_ge(S["w_ready"], b * 3 + 1)
                V.tensor_copy(convw[:, 0], convw_raw).then_inc(S["w_ready"], 1)
                dve.wait_ge(S["w_ready"], b * 3 + 2)
                V.tensor_tensor(convw[:, 1], convw_raw, convw[:, 0], ALU.subtract).then_inc(S["w_ready"], 1)

                def normalise_x1(c, s, n):
                    t = x1t[:, s, 0:n, :]
                    if isinstance(c, int):
                        dve.wait_ge(xc_in[s], b * (16 * (5 - s)) + 16 * (c // 2 + 1) - (0 if s == 0 else 0))
                    else:
                        dve.wait_ge(xc_in[s], b * (16 * (5 - s)) + 8 * c + (16 - 8 * s))
                    V.tensor_scalar(t[:, :, 1:1 + W], t[:, :, 1:1 + W], gn2[:, 11:12], gn2[:, 12:13],
                                    ALU.mult, ALU.add).then_inc(S["xc_pad"], 1)
                    dve.wait_ge(S["xc_pad"], b * (NCHUNK + 1) + c + 1)
                    V.tensor_copy(t[:, :, 0:1], t[:, :, 2:3])
                    V.tensor_copy(t[:, :, W + 1:W + 2], t[:, :, W - 1:W])
                    V.tensor_copy(t[:, :, W + 2:W + 3], t[:, :, W - 2:W - 1])
                    V.tensor_copy(t[:, :, W + 3:W + 4], t[:, :, 3:4]).then_inc(S["xc_n"], 1)

                with dve.Fori(0, NCHUNK // 2) as i:
                    for k in range(2):
                        normalise_x1(2 * i + k, k, 8)
                        if more:
                            for e in range(2):
                                pair_stats(b + 1, 4 * i + (2 * k + e), e)
                normalise_x1(NCHUNK, 0, 1)
                if more:
                    finish_stats1(b + 1)

            batches(dve, body)

        @block.tensor
        def _(pe):
            T = nc.tensor
            pe.wait_ge(S["g_ready"], 1)
            for j in range(2):
                for n in range(4):
                    t, k = n // 2, n % 2
                    ins = T.matmul(psum[:, j, :], dft[:, t, k, 128 * j:128 * j + 128], kern[:, t, k, :],
                                   start=n == 0, stop=n == 3)
            ins.then_inc(S["setup_p_mm"], 1)

            def stats_sums1(b):
                pe.wait_ge(S["st1_v"], b * 3 + 1)
                T.matmul(psum[:, 6, 0:2 * NPAIR], ones[:, :], mv1[:, :, :].rearrange("p g s -> p (g s)"),
                         start=True, stop=True).then_inc(S["st1_p"], 1)
                pe.wait_ge(S["st1_v"], b * 3 + 2)
                T.matmul(psum[:, 6, 64:64 + NPAIR], ones[:, :], gn1[:, 2, :], start=True, stop=True)\
                    .then_inc(S["st1_p"], 1)

            stats_sums1(0)

            def body(b, more):
                pe.wait_ge(S["g_ready"], 2)
                with pe.Fori(0, NPAIR // 2) as i:
                    pe.wait_ge(S["cv_free"], b * NOUT + SLOTS)
                    for k in range(2):
                        pe.wait_ge(S["raw_lo"], b * NPAIR + 2 * i + (k + 3))
                        for e in range(2):
                            s = 2 * k + e
                            pe.wait_ge(S["s1_free"], b * C + 4 * i + (s + 1))
                            for wb in range(NB):
                                n = 0
                                for kb in range(NB):
                                    for xt, gt in ((0, 0), (0, 1), (1, 0)):
                                        ins = T.matmul(psum[:, 2 * s + wb, :],
                                                       split[:, k, xt, e, kb, 128 * wb:128 * wb + 128],
                                                       G[:, gt, kb, 256:768], start=n == 0, stop=n == 5)
                                        n += 1
                            ins.then_inc(S["s1_mm"], 1)

                pe.wait_ge(S["z_pad"], (b + 1) * 4)
                pe.wait_ge(S["s1_free"], (b + 1) * C + SLOTS)

                def transform(u, s, n):
                    pe.wait_ge(S["s2_free"], b * NUNIT + u + 1)
                    for j in range(n):
                        m = 0
                        for wb in range(NB):
                            for ri in range(2):
                                for zt, gt in ((0, 0), (0, 1), (1, 0)):
                                    lhs = Zflat[:, 4 * zt + 2 * wb + ri, bass.ds((2 * u + j) * P, P)]
                                    rhs = G[:, gt, wb, 256 - 256 * ri:768 - 256 * ri]
                                    ins = T.matmul(psum[:, 2 * s + j, :], lhs, rhs, start=m == 0, stop=m == 11)
                                    m += 1
                    ins.then_inc(S["s2_mm"], 1)

                def mix(u, s, n):
                    pe.wait_ge(S["ang_done"], b * NUNIT + u + 1)
                    T.matmul(psum[:, 2 * s, 0:256 * n], mixw[:, 0, :], mag[:, s, 0:n].rearrange("p j w -> p (j w)"),
                             start=True, stop=False)
                    T.matmul(psum[:, 2 * s, 0:256 * n], mixw[:, 1, :], ang[:, s, 0:n].rearrange("p j w -> p (j w)"),
                             start=False, stop=True).then_inc(S["mix_mm"], 1)

                def step(u, s, n):
                    if n:
                        transform(u, s, n)
                    if not isinstance(u, int) or u >= 2:
                        mix(u - 2, (s + 2) % 4, blocks_of(u - 2))

                walk(pe, step, 2)

                pe.wait_ge(S["gn2_v"], b * 4 + 1)
                T.matmul(psum[:, 7, 0:2], quadm[:, :], gn2[:, 0:2], start=True, stop=True).then_inc(S["gn2_p"], 1)
                pe.wait_ge(S["gn2_v"], b * 4 + 2)
                T.matmul(psum[:, 7, 2:3], quadm[:, :], gn2[:, 7:8], start=True, stop=True).then_inc(S["gn2_p"], 1)
                pe.wait_ge(S["gn2_v"], b * 4 + 4)
                T.matmul(psum[:, 7, 3:4], ones[:, :], wmax[:, 1:2], start=True, stop=True).then_inc(S["gn2_p"], 1)


                def pair(c, k):
                    pe.wait_ge(S["cv_free"], b * NOUT + 4 * c + (k + 1))
                    n = 0
                    for kb in range(2):
                        for kx in range(KT):
                            for xt, wt in ((0, 0), (1, 0), (0, 1)):
                                ins = T.matmul(psum[:, k, :], convw[:, wt, kb, kx, :],
                                               conv_in[:, xt, bass.ds(8 * c + (2 * k + kb), 2), 4 - kx:4 - kx + W],
                                               start=n == 0, stop=n == 29)
                                n += 1
                    ins.then_inc(S["cv_mm"], 1)

                def chunk(c):
                    pe.wait_ge(S["w_ready"], b * 3 + 3)
                    pe.wait_ge(S["xc_lo"], b * (NCHUNK + 1) + c + 1)
                    for k in range(3):
                        pair(c, k)
                    pe.wait_ge(S["xc_lo"], b * (NCHUNK + 1) + c + 2)
                    pair(c, 3)

                with pe.Fori(0, NCHUNK) as c:
                    chunk(c)
                if more:
                    stats_sums1(b + 1)

            batches(pe, body)


def kernel(**inputs):
    import concourse.bacc as bacc
    from concourse.bass_utils import run_bass_kernel_spmd

    f32 = mybir.dt.float32
    x = np.ascontiguousarray(inputs["x"])
    B, C, H, W = x.shape
    Q = P // C
    w0 = np.asarray(inputs["L0_conv_w"])
    w1 = np.asarray(inputs["L1_conv_weight"])
    KT = w1.shape[-1]

    mix_w = np.zeros((P, 2, P), w0.dtype)
    for q in range(Q):
        for part in range(2):
            mix_w[q * C:(q + 1) * C, part, q * C:(q + 1) * C] = w0[:, part * C:(part + 1) * C].T
    conv_w = np.zeros((P, 2, KT, P), w1.dtype)
    tap = np.zeros((P, 2, P), np.float32)
    for q in range(Q):
        for ky in range(KT):
            kb, qi = divmod(q + 4 - ky, Q)
            for kx in range(KT):
                conv_w[qi * C:(qi + 1) * C, kb, kx, q * C:(q + 1) * C] = w1[:, :, ky, kx].T
        kb, qi = divmod(q + 1, Q)
        tap[qi * C:(qi + 1) * C, kb, q * C:(q + 1) * C] = np.eye(C, dtype=np.float32)
    group = (np.arange(P) % C) // 2
    quad_mean = ((group[:, None] == group[None, :]) / (2.0 * Q)).astype(np.float32)
    n = np.arange(W)
    pos = np.minimum(n, W - n).astype(np.float64) ** 2
    frq = (n - W // 2).astype(np.float64) ** 2
    grid_sq = np.concatenate([pos.reshape(2, P).T, frq.reshape(2, P).T, np.tile(pos, (P, 1))], axis=1).astype(np.float32)
    turn = 2 * np.pi * (np.outer(n, n) % W) / W
    arrays = {
        "x": x, "alpha": np.asarray(inputs["L0_conv_alpha"]).reshape(1, 1), "grid_sq": grid_sq,
        "dft_cos": np.cos(turn).astype(np.float32), "dft_sin": np.sin(turn).astype(np.float32),
        "mix_w": mix_w, "conv_w": conv_w, "tap": tap, "quad_mean": quad_mean,
    }
    nc = bacc.Bacc("TRN2", target_bir_lowering=False, num_devices=1)
    args = [nc.dram_tensor(k, a.shape, f32, kind="ExternalInput").ap() for k, a in arrays.items()]
    args.append(nc.dram_tensor("out", x.shape, f32, kind="ExternalOutput").ap())
    args.append(nc.dram_tensor("x1_dram", (B, P, H // Q + 1, W), f32, kind="Internal").ap())
    frft_conv_kernel(nc, *args)
    r = run_bass_kernel_spmd(nc, [arrays], core_ids=[0])
    return r.results[0]["out"]
```

```python
from contextlib import ExitStack

import numpy as np

import concourse.bass as bass
from concourse import mybir


P = 128
F32 = mybir.dt.float32
F16 = mybir.dt.float16
I32 = mybir.dt.int32
ALU = mybir.AluOpType
ACT = mybir.ActivationFunctionType
AX_X = mybir.AxisListType.X

PI = float(np.float32(np.pi))
PI_LOW = float(np.pi - np.float64(np.float32(np.pi)))
HALF_PI = float(np.float32(np.pi / 2))
HALF_PI_LOW = float(np.pi / 2 - np.float64(np.float32(np.pi / 2)))
TWO_PI_A = 6.28125
TWO_PI_B = float(np.float32(2 * np.pi - TWO_PI_A))
TWO_PI_C = float(np.float32(2 * np.pi - TWO_PI_A - np.float64(np.float32(2 * np.pi - TWO_PI_A))))
ROUND = 12582912.0
X_SCALE = 64.0
G_SCALE = 4096.0
EPS = 1e-5


def frft_conv_kernel(nc, x, alpha, grid_sq, dft_cos, dft_sin, mix_w, conv_w, tap, quad_mean, out, x1_dram):
    B, C, H, W = x.shape
    Q = P // C
    NPAIR = C // 2
    NB = H // P
    EW, OW = W // 2 + 1, W // 2 - 1
    NBLK = H // Q + 1
    NUNIT = NBLK // 2 + 1
    HALF = NUNIT // 2
    ROWS = (HALF * 2 * Q, HALF * 2 * Q + Q)
    RMAX = ROWS[1]
    EXT = H + 4
    WP = W + 4
    KT = 5
    NOUT = H // Q // 2
    AHEAD = 3
    LINKS1 = 10
    LINKS2 = 14
    CB = 5
    assert P == Q * C and NB == 2 and NBLK == 65 and NUNIT == 33 and NOUT == 2 * HALF

    with ExitStack() as ctx:
        def sb(name, shape, dt=F32):
            return ctx.enter_context(nc.sbuf_tensor(name, shape, dt))

        psum = ctx.enter_context(nc.psum_tensor("psum", [P, 8, 512], F32))

        arena = sb("arena", [P, 8 * RMAX * C // 2])
        Zflat = arena[:, :].bitcast(F16).rearrange("p (l n) -> p l n", l=8)
        Z = arena[:, :].bitcast(F16).rearrange("p (t k r c) -> p t k r c", t=2, k=4, c=C)
        dft = arena[:, 0:1024].rearrange("p (s k m) -> p s k m", s=2, k=2)
        kern = arena[:, 1024:3072].rearrange("p (s k n) -> p s k n", s=2, k=2)
        part_tmp = arena[:, 3072:6144].rearrange("p (i n) -> p i n", n=256)
        parts = arena[:, 6144:7680].rearrange("p (j n) -> p j n", j=3)
        g_sum = arena[:, 7680:8192]
        grid = arena[:, 8192:8712].rearrange("p (i n) -> p i n", i=2)

        Zmid = sb("Zmid", [P, RMAX * C], F16)
        Grow = sb("Grow", [P, 2, NB, 2, EXT], F16)
        Gcol = sb("Gcol", [P, 2, 3 * (EW + OW)], F16)
        Gmid = sb("Gmid", [P, 2 * EW], F16)
        neg_mid = sb("neg_mid", [1, 2, EW], F16)
        mixw = sb("mixw", [P, 2, P])
        convw = sb("convw", [P, 2, 2, KT, P], F16)
        convw_raw = sb("convw_raw", [P, 2, KT, P])
        middle = sb("middle", [P, 2, P])
        tapm = sb("tapm", [P, 2, P])
        quadm = sb("quadm", [P, P])
        ones = sb("ones", [P, P])
        tiny = sb("tiny", [P, 1])
        raw = sb("raw", [P, 2, 2, NB, W])
        fold = sb("fold", [P, 2, 2, 2, NB, P])
        split = sb("split", [P, 4, 2, 2, 2, NB, P], F16)
        res = sb("res", [P, 4, 2, W])
        trf = sb("trf", [P, 4, 2, 2, W])
        odd = sb("odd", [P, 2, 2, 2 * OW])
        sq = sb("sq", [P, 2, 2, 2, W])
        mag = sb("mag", [P, 4, 2, W])
        ang = sb("ang", [P, 4, 2, W])
        stat_in = sb("stat_in", [P, 2, 2 * W])
        x1t = sb("x1t", [P, CB, WP])
        conv_in = sb("conv_in", [P, 2, 2, CB, WP], F16)
        outs = sb("outs", [P, 2, 2, W])

        ang_s = sb("ang_s", [P, 3, 3])
        sc = sb("sc", [P, 16])
        bst1 = sb("bst1", [P, C, 6])
        mv1 = sb("mv1", [P, NPAIR, 2])
        gn1 = sb("gn1", [P, 6, NPAIR])
        bst2 = sb("bst2", [P, NBLK, 6])
        gn2 = sb("gn2", [P, 16])
        wmax = sb("wmax", [P, 3])

        names = """primed consts_in first_in0 first_in1 parts_done gcol_hi gcol_lo gcol_ready setup_p setup_v setup_a setup_mm g_ready mid_in link raw_in0 raw_in1 norm_done raw_n raw_hi raw_lo
            s1_mm s1_free z_hi zmid_in s2_mm y_free odd_done sq_done sum_done r_done d_done rec_done u_done at_done
            sgn_done ang_done mix_mm x1_done st2_done res_in0 res_in1 res_in2 res_in3 x1_out0 x1_out1 x1_out2 x1_out3
            st_in0 st_in1 st1_done st1_v st1_p st1_a gn2_v gn2_p gn2_a w_in w_ready link1 link2
            xc_in xc_pad xc_n xc_hi xc_lo cv_mm cv_free cv_out0 cv_out1""".split()
        S = {n: ctx.enter_context(nc.semaphore(n)) for n in names}
        raw_in = [S["raw_in0"], S["raw_in1"]]
        res_in = [S[f"res_in{i}"] for i in range(4)]
        x1_out = [S[f"x1_out{i}"] for i in range(4)]
        st_in = [S["st_in0"], S["st_in1"]]
        first_in = [S["first_in0"], S["first_in1"]]
        cv_out = [S["cv_out0"], S["cv_out1"]]

        x_rows = x.rearrange("b c (k p) w -> b p c k w", p=P)
        x_stat = x.rearrange("b c (p r) w -> b p c (r w)", p=P)

        sums1 = psum[:, 5, 192:192 + 2 * NPAIR]
        sums1_sq = psum[:, 5, 224:224 + NPAIR]
        sums2 = psum[:, 5, 240:244]
        def rows_of(s, n):
            return psum[:, 2 * s:2 * s + 2, :].rearrange("p j (i r) -> p (j i) r", i=2)[:, :, 0:n]

        PRIME = {"raw_n": 2, "raw_lo": 2, "s1_free": 4, "y_free": 2, "cv_free": 2, "cv_out0": 64, "cv_out1": 64,
                 "st1_done": 2, "xc_lo": 1, "w_ready": 1, "x1_out0": 16, "x1_out1": 16, "x1_out2": 16, "x1_out3": 16}

        def wait(eng, name, n):
            eng.wait_ge(S[name], n + PRIME.get(name, 0))

        class Pair:

            def __init__(self, p, j, c, k):
                self.p, self.j, self.c, self.k = p, j, c, k

        def walk(eng, step, n, start, ahead):
            for u, pair in ((0, Pair(0, 0, 0, 0)), (1, Pair(1, 1, 0, 0)), (2, None)):
                start(u)
                step(u, u, pair)
            with eng.Fori(0, 3) as i:
                for q in range(4):
                    step(4 * i + (q + 3), (q + 3) % 4,
                         Pair(4 * i + (q + 2), q % 2, 2 * i + (1 + q // 2), (1 + q // 2) % 2))
            for u in range(15, n + 3):
                ahead(u - 15)
                step(u, u % 4, Pair(u - 2, u % 2, HALF // 2 - 1, 1) if HALF <= u < HALF + 2 else None)

        class Half:

            def __init__(self, b, h, conv, stats):
                self.b, self.h, self.conv, self.stats = b, h, conv, stats
                self.n = HALF + h
                self.first = b * NUNIT + HALF * h
                self.pairs = (b * 2 + h) * NPAIR
                self.chans = (b * 2 + h) * C
                self.rows = ROWS[h]

            def has(self, v):
                return not isinstance(v, int) or 0 <= v < self.n

            def blocks(self, v):
                return 1 if isinstance(v, int) and v == HALF else 2

            def next_chunk(self, pair):
                if pair is None or not self.conv or pair.j or (self.h and isinstance(pair.c, int) and pair.c == HALF // 2 - 1):
                    return None
                return pair.c + (HALF // 2 * self.h + 1)

            def stat(self, u):
                p = u - 3
                if not self.stats or self.h or (isinstance(p, int) and not 0 <= p < HALF):
                    return None
                return p

        def batches(eng, half, last_conv):
            def batch(b, conv, stats):
                half(Half(b, 0, conv, stats))
                half(Half(b, 1, conv, stats))

            batch(0, False, True)
            with eng.Fori(1, B - 1) as b:
                batch(b, True, True)
            batch(B - 1, True, False)
            last_conv()

        def after(hf):
            if hf.h == 0:
                return Half(hf.b, 1, hf.conv, hf.stats)
            return Half(hf.b + 1, 0, True, True) if hf.stats else None

        GCOL = ((0, 0, EW), (3 * EW, 1, OW))

        def gcol_part(j):
            base, first, n = GCOL[j]
            part = parts[:, j, :].rearrange("p (i n) -> p i n", i=2)[:, :, first:first + n]
            return (part, *(Gcol[:, t, base + n:base + 3 * n].rearrange("p (i n) -> p i n", i=2) for t in range(2)))

        def minus_im(j):
            base, _, n = GCOL[j]
            return [Gcol[:, t, base:base + n] for t in range(2)]

        def four_channels(k):
            return trf[:, 2 * k:2 * k + 2].rearrange("p s b i w -> p (s b) (i w)")

        block = ctx.enter_context(nc.Block())

        @block.sync
        def _(sp):
            sp.dma_start(grid[:, 0, :], grid_sq).then_inc(S["consts_in"], 16)
            sp.dma_start(sc[:, 0:1], alpha.to_broadcast([P, 1])).then_inc(S["consts_in"], 16)
            sp.dma_start(dft[:, 0, :, :], dft_cos.rearrange("(k p) m -> p k m", p=P)).then_inc(S["consts_in"], 16)
            sp.dma_start(dft[:, 1, :, :], dft_sin.rearrange("(k p) m -> p k m", p=P)).then_inc(S["consts_in"], 16)
            sp.dma_start(mixw[:, :, :], mix_w).then_inc(S["consts_in"], 16)
            sp.dma_start(tapm[:, :, :], tap).then_inc(S["consts_in"], 16)
            sp.dma_start(quadm[:, :], quad_mean).then_inc(S["consts_in"], 16)
            sp.dma_start(convw_raw[:, :, :, :], conv_w).then_inc(S["w_in"], 16)

            def load_stats(b, p):
                wait(sp, "st1_done", b * C + 2 * p)
                for k in range(2):
                    sp.dma_start(stat_in[:, k, :], x_stat[bass.ds(b, 1), :, bass.ds(2 * p + k, 1), :]
                                 .rearrange("b p c n -> (b p) (c n)")).then_inc(st_in[k], 16)

            def load_raw(hf, g, k, free=False):
                if not free:
                    wait(sp, "raw_n", hf.pairs + g - 1)
                sp.dma_start(raw[:, k, :, :, :], x_rows[bass.ds(hf.b, 1), :, bass.ds(2 * g, 2), :, :]
                             .rearrange("b p c k w -> (b p) c k w")).then_inc(raw_in[k], 16)

            sp.wait_ge(S["primed"], 1)
            for g in range(C // 4):
                if g >= 2:
                    wait(sp, "st1_done", 4 * (g - 1))
                sp.dma_start(four_channels(g % 2), x_stat[0, :, 4 * g:4 * g + 4, :]).then_inc(first_in[g % 2], 16)

            sp.wait_ge(S["g_ready"], 2)
            sp.wait_ge(S["setup_p"], 1)
            for r, (t, im) in enumerate(((0, 0), (0, 0), (1, 0), (0, 1), (0, 1), (1, 1))):
                first = neg_mid[0:1, t, :] if im else Grow[0:1, t, 1, 0, 1:1 + EW]
                second = Grow[0:1, t, 1, 0 if im else 1, 1:1 + EW]
                sp.dma_start(Gmid[r:r + 1, 0:EW], first).then_inc(S["mid_in"], 16)
                sp.dma_start(Gmid[r:r + 1, EW:2 * EW], second).then_inc(S["mid_in"], 16)

            def load_res(hf, u, s):
                b, h = hf.b, hf.h
                per = 9 if s == 0 else 8
                wait(sp, f"x1_out{s}", b * (16 * per) + 64 * h + 4 * (u - s))
                for q in range(Q):
                    row = 8 * u + (q - 1 + 8 * HALF * h)
                    if isinstance(u, int) and u == 0 and h == 0 and q == 0:
                        rows = x[bass.ds(b, 1), :, 1:4:2, :]
                    elif isinstance(u, int) and u == HALF:
                        r = [H - 1, H - 2, H - 3, 2][q]
                        rows = x[bass.ds(b, 1), :, r:r + 1, :]
                    else:
                        rows = x[bass.ds(b, 1), :, bass.ds(row, 2, step=4), :]
                    sp.dma_start(res[C * q:C * q + C, s, 0:hf.blocks(u), :], rows.rearrange("b c r w -> (b c) r w"))\
                      .then_inc(res_in[s], 16)

            def load_chunk(cb, e):
                wait(sp, "xc_lo", cb * HALF + e)
                sp.dma_start(x1t[:, :, 1:1 + W], x1_dram[bass.ds(cb, 1), :, bass.ds(4 * e, CB), :]
                             .rearrange("b p j w -> (b p) j w")).then_inc(S["xc_in"], 16)

            def store_out(cb, p, k):
                wait(sp, "cv_free", cb * NOUT + p + 1)
                for q in range(Q):
                    sp.dma_start(out[bass.ds(cb, 1), :, bass.ds(8 * p + q, 2, step=4), :]
                                 .rearrange("b c r w -> (b c) r w"), outs[C * q:C * q + C, k, :, :])\
                      .then_inc(cv_out[k], 16)

            def start_conv(cb):
                for s in range(4):
                    wait(sp, f"x1_out{s}", (cb + 1) * (16 * (9 if s == 0 else 8)))
                load_chunk(cb, 0)

            def pre(hf):
                load_raw(hf, 1, 1)
                load_raw(hf, 0, 0, free=True)

            def ahead(hf, k):
                if hf and k in (1, 2):
                    load_raw(hf, k + 1, k - 1)

            def half(hf):
                b = hf.b
                with sp.Fori(0, NPAIR // 2 - 2) as i:
                    for k in range(2):
                        load_raw(hf, 2 * i + (k + 4), k)
                if hf.h == 0 and hf.conv:
                    start_conv(b - 1)
                load_res(hf, 0, 0)
                sp.wait_ge(S["s1_free"], hf.chans + C + 4)
                for r, (t, ri) in enumerate(((0, 0), (1, 0), (0, 0), (0, 1), (1, 1), (0, 1))):
                    sp.dma_start(Zmid[r:r + 1, 0:hf.rows * C], Zflat[0:1, 4 * t + 2 + ri, 0:hf.rows * C])\
                      .then_inc(S["zmid_in"], 16)

                def step(u, s, pair):
                    e = hf.next_chunk(pair)
                    if e is not None:
                        load_chunk(b - 1, e)
                    if hf.stat(u) is not None:
                        load_stats(b + 1, u - 3)
                    if hf.has(u - 1) and not (isinstance(u, int) and u == 1):
                        load_res(hf, u - 1, (s + 3) % 4)
                    if hf.has(u - 3):
                        v, t, m = u - 3, (s + 1) % 4, hf.blocks(u - 3)
                        sp.wait_ge(S["x1_done"], hf.first + v + 1)
                        sp.dma_start(x1_dram[bass.ds(b, 1), :, bass.ds(2 * v + 2 * HALF * hf.h, m), :]
                                     .rearrange("b p j w -> (b p) j w"), res[:, t, 0:m, :]).then_inc(x1_out[t], 16)
                    if pair is not None and hf.conv:
                        store_out(b - 1, pair.p + HALF * hf.h, pair.j)
                    if isinstance(u, int) and u == 2 and after(hf):
                        pre(after(hf))

                walk(sp, step, hf.n, lambda k: None, lambda k: ahead(after(hf), k))

            def last():
                start_conv(B - 1)
                with sp.Fori(0, HALF - 1) as i:
                    load_chunk(B - 1, i + 1)
                    for k in range(2):
                        store_out(B - 1, 2 * i + k, k)
                for k in range(2):
                    store_out(B - 1, NOUT - 2 + k, k)
                for k in range(2):
                    wait(sp, f"cv_out{k}", B * HALF * 64)

            pre(Half(0, 0, False, True))
            for k in range(4):
                ahead(Half(0, 0, False, True), k)
            batches(sp, half, last)

        @block.gpsimd
        def _(pool):
            for name, n in PRIME.items():
                pool.sem_inc(S[name], n)
            pool.sem_inc(S["primed"], 1)
            nc.gpsimd.memset(Zmid[:, :], 0.0)
            nc.gpsimd.memset(Gmid[:, :], 0.0).then_inc(S["setup_p"], 1)

            pool.wait_ge(S["gcol_hi"], 1)
            for j in range(2):
                part, hi, lo = gcol_part(j)
                ins = nc.gpsimd.tensor_tensor(lo, part, hi, ALU.subtract)
            ins.then_inc(S["gcol_lo"], 1)

            def pair_lo(hf, g, k):
                pool.wait_ge(S["raw_hi"], hf.pairs + g + 1)
                nc.gpsimd.tensor_tensor(split[:, k, 1], fold[:, k % 2], split[:, k, 0], ALU.subtract)\
                    .then_inc(S["raw_lo"], 1)

            def ahead(hf, k):
                if hf and k < 2:
                    pair_lo(hf, k, k)

            def chunk_lo(cb, e, k):
                pool.wait_ge(S["xc_hi"], cb * HALF + e + 1)
                nc.gpsimd.tensor_tensor(conv_in[:, k, 1], x1t[:, :, :], conv_in[:, k, 0], ALU.subtract)\
                    .then_inc(S["xc_lo"], 1)

            def half(hf):
                pair_lo(hf, 2, 2)
                with pool.Fori(0, NPAIR // 4 - 1) as i:
                    for k in range(4):
                        pair_lo(hf, 4 * i + (k + AHEAD), (k + AHEAD) % 4)
                pair_lo(hf, NPAIR - 1, 3)
                if hf.h == 0 and hf.conv:
                    chunk_lo(hf.b - 1, 0, 0)

                def step(u, s, pair):
                    if hf.has(u):
                        n = hf.blocks(u)
                        pool.wait_ge(S["sq_done"], hf.first + u + 1)
                        nc.gpsimd.tensor_tensor(sq[:, s % 2, 0, 0:n], sq[:, s % 2, 0, 0:n], sq[:, s % 2, 1, 0:n], ALU.add)\
                            .then_inc(S["sum_done"], 1)
                    if hf.has(u - 1):
                        v, t, m = u - 1, (s + 3) % 4, hf.blocks(u - 1)
                        pool.wait_ge(S["rec_done"], hf.first + v + 1)
                        nc.gpsimd.tensor_tensor(ang[:, t, 0:m], trf[:, t, 0:m, 0, :], sq[:, t % 2, 0, 0:m], ALU.mult)\
                            .then_inc(S["u_done"], 1)
                    if hf.has(u):
                        pool.wait_ge(S["r_done"], hf.first + u + 1)
                        nc.gpsimd.tensor_tensor(sq[:, s % 2, 0, 0:n], sq[:, s % 2, 1, 0:n], mag[:, s, 0:n], ALU.add)\
                            .then_inc(S["d_done"], 1)
                    e = hf.next_chunk(pair)
                    if e is not None:
                        chunk_lo(hf.b - 1, e, 1 - pair.k)

                walk(pool, step, hf.n, lambda k: None, lambda k: ahead(after(hf), k))

            def last():
                chunk_lo(B - 1, 0, 0)
                with pool.Fori(0, HALF // 2 - 1) as i:
                    chunk_lo(B - 1, 2 * i + 1, 1)
                    chunk_lo(B - 1, 2 * i + 2, 0)
                chunk_lo(B - 1, HALF - 1, 1)

            for k in range(4):
                ahead(Half(0, 0, False, True), k)
            batches(pool, half, last)

        @block.scalar
        def _(act):
            A = nc.scalar
            act.wait_ge(S["setup_v"], 1)
            A.activation(grid[:, 0, :], grid[:, 1, :], ACT.Sin).then_inc(S["setup_a"], 1)
            act.wait_ge(S["setup_v"], 2)
            A.activation(grid[:, 1, :], grid[:, 1, :], ACT.Sin).then_inc(S["setup_a"], 1)

            act.wait_ge(S["parts_done"], 1)
            for j in range(2):
                part, hi, lo = gcol_part(j)
                ins = A.copy(hi, part)
            ins.then_inc(S["gcol_hi"], 1)
            act.wait_ge(S["gcol_lo"], 1)
            for j in range(2):
                _, hi, lo = gcol_part(j)
                for im, to in zip((hi[:, 1, :], lo[:, 1, :]), minus_im(j)):
                    ins = A.activation(to, im, ACT.Copy, scale=-1.0)
            ins.then_inc(S["gcol_ready"], 1)

            def root_of_variance1(b):
                act.wait_ge(S["st1_v"], b * 3 + 3)
                A.activation(gn1[:, 3, :], gn1[:, 1, :], ACT.Sqrt).then_inc(S["st1_a"], 1)

            def root_of_variance2(cb):
                act.wait_ge(S["gn2_v"], cb * 4 + 3)
                A.activation(gn2[:, 5:6], gn2[:, 4:5], ACT.Sqrt).then_inc(S["gn2_a"], 1)

            def pair_hi(hf, g, k):
                wait(act, "raw_n", hf.pairs + g + 1)
                A.copy(split[:, k, 0], fold[:, k % 2]).then_inc(S["raw_hi"], 1)

            def normalise(hf, g, k):
                act.wait_ge(S["link1"], (hf.b + 1) * LINKS1)
                act.wait_ge(raw_in[k], (hf.pairs + g) * 8 + (16 - 8 * k))
                for c in range(2):
                    A.activation(raw[:, k, c], raw[:, k, c], ACT.Identity, bias=gn1[:, 5, bass.ds(g, 1)],
                                 scale=gn1[:, 4, bass.ds(g, 1)]).then_inc(S["norm_done"], 1)

            def chunk_hi(cb, e, k):
                act.wait_ge(S["xc_n"], cb * HALF + e + 1)
                A.copy(conv_in[:, k, 0], x1t[:, :, :]).then_inc(S["xc_hi"], 1)

            def rows_out(cb, p, k, before):
                act.wait_ge(S["cv_mm"], cb * NOUT + p + 1)
                wait(act, f"cv_out{k}", cb * (HALF * 64) + before * 64)
                A.activation(outs[:, k, :, :], psum[:, 6 + k, :].rearrange("p (j w) -> p j w", j=2),
                             ACT.Identity, bias=gn2[:, 8:9], scale=gn2[:, 9:10]).then_inc(S["cv_free"], 1)

            def ahead(hf, k):
                if hf and k == 0:
                    normalise(hf, 0, 0)
                    normalise(hf, 1, 1)
                    pair_hi(hf, 0, 0)
                if hf and k == 1:
                    pair_hi(hf, 1, 1)
                if hf and k == 2:
                    normalise(hf, 2, 0)

            def half(hf):
                def product_hi(c, s):
                    act.wait_ge(S["s1_mm"], hf.chans + c + 1)
                    A.activation(Z[:, 0, :, 0:hf.rows, bass.ds(c, 1)].rearrange("p k r c -> p k (r c)"),
                                 rows_of(s, hf.rows), ACT.Copy, scale=1.0 / G_SCALE).then_inc(S["z_hi"], 1)

                def pair(g, k):
                    for e in range(2):
                        product_hi(2 * g + e, (2 * k + e) % 4)
                    pair_hi(hf, g + AHEAD, (k + AHEAD) % 4)
                    if not isinstance(g, int) or g + AHEAD + 1 < NPAIR:
                        normalise(hf, g + (AHEAD + 1), (k + AHEAD + 1) % 2)

                pair_hi(hf, 2, 2)
                normalise(hf, 3, 1)
                turns = 1 if hf.h == 0 and hf.conv else 0
                for k in range(4 * turns):
                    pair(k, k)
                if turns:
                    root_of_variance2(hf.b - 1)
                with act.Fori(turns, NPAIR // 4 - 1) as i:
                    for k in range(4):
                        pair(4 * i + k, k)
                pair(NPAIR - 4, 0)
                if hf.h == 0 and hf.conv:
                    chunk_hi(hf.b - 1, 0, 0)
                for c in range(C - 2 * AHEAD, C):
                    product_hi(c, c % 4)

                def step(u, s, pair):
                    if hf.has(u):
                        n = hf.blocks(u)
                        act.wait_ge(S["s2_mm"], hf.first + u + 1)
                        k = 2 * (s % 2)
                        A.copy(odd[:, s % 2, 0:n, :], psum[:, k:k + n, 2 * EW:512])
                        A.copy(trf[:, s, 0:n, :, 0:EW:EW - 1], psum[:, k:k + n, 0:2 * EW]
                               .rearrange("p j (i w) -> p j i w", i=2)[:, :, :, 0:EW:EW - 1]).then_inc(S["odd_done"], 1)
                    if hf.has(u - 2):
                        v, t, m = u - 2, (s + 2) % 4, hf.blocks(u - 2)
                        act.wait_ge(S["u_done"], hf.first + v + 1)
                        A.activation(ang[:, t, 0:m], ang[:, t, 0:m], ACT.Arctan).then_inc(S["at_done"], 1)
                        A.activation(trf[:, t, 0:m, 1, :], trf[:, t, 0:m, 1, :], ACT.Sign).then_inc(S["sgn_done"], 1)
                    if hf.has(u):
                        wait(act, "y_free", hf.first + u + 1)
                        A.activation(sq[:, s % 2, 0, 0:n], trf[:, s, 0:n, 0, :], ACT.Square)
                        A.activation(sq[:, s % 2, 1, 0:n], trf[:, s, 0:n, 1, :], ACT.Square).then_inc(S["sq_done"], 1)
                        act.wait_ge(S["sum_done"], hf.first + u + 1)
                        A.activation(mag[:, s, 0:n], sq[:, s % 2, 0, 0:n], ACT.Sqrt, bias=tiny[:, 0:1])
                        A.activation(sq[:, s % 2, 1, 0:n], trf[:, s, 0:n, 1, :], ACT.Abs).then_inc(S["r_done"], 1)
                    e = hf.next_chunk(pair)
                    if e is not None:
                        chunk_hi(hf.b - 1, e, 1 - pair.k)
                    if pair is not None and hf.conv:
                        rows_out(hf.b - 1, pair.p + HALF * hf.h, pair.j, pair.c + HALF // 2 * hf.h)

                def start(k):
                    if k == 2 and hf.h == 1 and hf.stats:
                        root_of_variance1(hf.b + 1)

                walk(act, step, hf.n, start, lambda k: ahead(after(hf), k))

            def last():
                root_of_variance2(B - 1)
                chunk_hi(B - 1, 0, 0)
                with act.Fori(0, HALF // 2 - 1) as i:
                    for k in range(2):
                        chunk_hi(B - 1, 2 * i + (k + 1), 1 - k)
                        for e in range(2):
                            rows_out(B - 1, 4 * i + (2 * k + e), e, 2 * i + k)
                chunk_hi(B - 1, HALF - 1, 1)
                for k in range(4):
                    rows_out(B - 1, NOUT - 4 + k, k % 2, HALF - 2 + k // 2)

            root_of_variance1(0)
            for k in range(4):
                ahead(Half(0, 0, False, True), k)
            batches(act, half, last)

        @block.vector
        def _(dve):
            V = nc.vector
            chain = [0]

            def link(ins):
                chain[0] += 1
                ins.then_inc(S["link"], 1)
                dve.wait_ge(S["link"], chain[0])

            def first_stats(groups):
                for g in groups:
                    dve.wait_ge(first_in[g % 2], 16 * (g // 2) + 16)
                    for c in range(4):
                        V.bn_stats(bst1[:, 4 * g + c, :], four_channels(g % 2)[:, c, :]).then_inc(S["st1_done"], 1)

            V.memset(ones[:, :], 1.0 / P)
            V.memset(tiny[:, :], 2.0 ** -60)
            dve.wait_ge(S["consts_in"], 16 * 7)
            a = sc[:, 1:2]
            link(V.tensor_scalar(a, sc[:, 0:1], float(np.float32(1e-4)), float(np.float32(2.0 - 1e-4)), ALU.max, ALU.min))
            y, z, acc = ang_s[:, 0, :], ang_s[:, 1, :], ang_s[:, 2, :]
            link(V.tensor_scalar(sc[:, 2:3], a, PI, None, ALU.mult))
            link(V.tensor_scalar(y[:, 0:1], sc[:, 2:3], 0.5, None, ALU.mult))
            link(V.tensor_scalar(y[:, 1:2], sc[:, 2:3], 0.25, None, ALU.mult))
            link(V.tensor_scalar(y[:, 2:3], y[:, 1:2], -1.0, HALF_PI, ALU.mult, ALU.add))
            link(V.tensor_scalar(y[:, 2:3], y[:, 2:3], HALF_PI_LOW, None, ALU.add))
            link(V.tensor_scalar(sc[:, 3:4], y[:, 0:1], -1.0, PI, ALU.mult, ALU.add))
            link(V.tensor_scalar(sc[:, 3:4], sc[:, 3:4], PI_LOW, None, ALU.add))
            link(V.tensor_tensor(y[:, 0:1], y[:, 0:1], sc[:, 3:4], ALU.min))
            link(V.tensor_tensor(z, y, y, ALU.mult))
            fact = [-1 / 6, 1 / 120, -1 / 5040, 1 / 362880, -1 / 39916800, 1 / 6227020800, -1 / 1307674368000]
            link(V.tensor_scalar(acc, z, fact[6], fact[5], ALU.mult, ALU.add))
            for f in fact[4::-1]:
                link(V.tensor_tensor(acc, acc, z, ALU.mult))
                link(V.tensor_scalar(acc, acc, f, None, ALU.add))
            link(V.tensor_tensor(acc, acc, z, ALU.mult))
            link(V.tensor_tensor(acc, acc, y, ALU.mult))
            link(V.tensor_tensor(acc, acc, y, ALU.add))
            link(V.reciprocal(sc[:, 4:5], acc[:, 2:3]))
            link(V.tensor_tensor(sc[:, 5:6], acc[:, 1:2], sc[:, 4:5], ALU.mult))
            link(V.tensor_scalar(sc[:, 6:7], acc[:, 0:1], float(W), None, ALU.mult))
            link(V.reciprocal(sc[:, 7:8], sc[:, 6:7]))
            link(V.tensor_scalar(sc[:, 8:9], acc[:, 0:1], 1e-12, None, ALU.add))
            link(V.reciprocal(sc[:, 9:10], sc[:, 8:9]))
            link(V.tensor_scalar(mixw[:, 0, :], mixw[:, 0, :], sc[:, 9:10], 1.0 / (X_SCALE * G_SCALE), ALU.mult, ALU.mult))
            link(V.tensor_scalar(mixw[:, 1, :], mixw[:, 1, :], -2.0 / float(np.pi), None, ALU.mult))
            th, kk = grid[:, 0, :], grid[:, 1, :]
            link(V.tensor_scalar(th, th, PI, None, ALU.mult))
            link(V.tensor_scalar(th[:, 0:2], th[:, 0:2], sc[:, 5:6], 1.0 / W, ALU.mult, ALU.mult))
            link(V.tensor_scalar(th[:, 4:260], th[:, 4:260], sc[:, 5:6], 1.0 / W, ALU.mult, ALU.mult))
            link(V.tensor_scalar(th[:, 2:4], th[:, 2:4], sc[:, 7:8], None, ALU.mult))
            link(V.tensor_scalar(kk, th, float(1 / (2 * np.pi)), ROUND, ALU.mult, ALU.add))
            link(V.tensor_scalar(kk, kk, ROUND, None, ALU.subtract))
            for part in (TWO_PI_A, TWO_PI_B, TWO_PI_C):
                link(V.scalar_tensor_tensor(th, kk, -part, th, ALU.mult, ALU.add))
            V.tensor_scalar(kk, th, 3.1415925, -3.1415925, ALU.min, ALU.max).then_inc(S["setup_v"], 1)
            dve.wait_ge(S["setup_a"], 1)
            dve.wait_ge(S["setup_v"], 1)
            link(V.scalar_tensor_tensor(kk, kk, -1.0, kk, ALU.mult, ALU.max))
            V.tensor_scalar(kk, kk, -1.0, HALF_PI, ALU.mult, ALU.add).then_inc(S["setup_v"], 1)
            dve.wait_ge(S["setup_a"], 2)
            sin_, cos_ = th, kk
            link(V.tensor_scalar(sc[:, 10:12], sin_[:, 2:4], -1.0, None, ALU.mult))
            for t in range(2):
                for k in range(2):
                    V.tensor_scalar(kern[:, t, k, 0:256], dft[:, t, k, :], cos_[:, 2 + k:3 + k], None, ALU.mult)
                    ins = V.tensor_scalar(kern[:, t, k, 256:512], dft[:, t, k, :], sc[:, 10 + k:11 + k], None, ALU.mult)
            ins.then_inc(S["g_ready"], 1)
            link(V.tensor_scalar(sc[:, 12:14], cos_[:, 0:2], G_SCALE / W, None, ALU.mult))
            link(V.tensor_scalar(sc[:, 14:16], sin_[:, 0:2], G_SCALE / W, None, ALU.mult))
            first_stats(range(0, 3))
            dve.wait_ge(S["w_in"], 16)
            V.tensor_copy(middle[:, :, :], convw_raw[:, :, 3, :])
            V.tensor_reduce(wmax[:, 2:3], convw_raw[:, :, :, :], mybir.AxisListType.XYZ, ALU.min)
            link(V.tensor_reduce(wmax[:, 0:1], convw_raw[:, :, :, :], mybir.AxisListType.XYZ, ALU.max))
            V.scalar_tensor_tensor(wmax[:, 0:1], wmax[:, 2:3], -1.0, wmax[:, 0:1], ALU.mult, ALU.max)
            dve.wait_ge(S["setup_mm"], 1)
            rc, rs = cos_[:, 4:260], sin_[:, 4:260]
            work = [[part_tmp[:, 4 * j + n, :] for n in range(4)] + [parts[:, j, 0:256], parts[:, j, 256:512]]
                    for j in range(3)]
            for j, (t0, t1, ur, ui, gr, gi) in enumerate(work):
                V.tensor_scalar(t0, psum[:, j, 0:256], sc[:, 12 + j // 2:13 + j // 2], None, ALU.mult)
                ins = V.tensor_scalar(t1, psum[:, j, 0:256], sc[:, 14 + j // 2:15 + j // 2], None, ALU.mult)
            link(ins)
            for j, (t0, t1, ur, ui, gr, gi) in enumerate(work):
                V.scalar_tensor_tensor(ur, psum[:, j, 256:512], sc[:, 14 + j // 2:15 + j // 2], t0, ALU.mult, ALU.add)
                ins = V.scalar_tensor_tensor(ui, psum[:, j, 256:512], sc[:, 12 + j // 2:13 + j // 2], t1,
                                             ALU.mult, ALU.subtract)
            link(ins)
            for t0, t1, ur, ui, gr, gi in work:
                V.tensor_tensor(gr, ur, rc, ALU.mult)
                V.tensor_tensor(t1, ui, rs, ALU.mult)
                V.tensor_tensor(gi, ui, rc, ALU.mult)
                ins = V.tensor_tensor(t0, ur, rs, ALU.mult)
            link(ins)
            for t0, t1, ur, ui, gr, gi in work:
                V.tensor_tensor(gr, gr, t1, ALU.add)
                ins = V.tensor_tensor(gi, gi, t0, ALU.subtract)
            ins.then_inc(S["parts_done"], 1)
            dve.wait_ge(S["parts_done"], 1)
            link(V.tensor_tensor(g_sum, parts[:, 0, :], parts[:, 1, :], ALU.add))
            rows = [full.rearrange("p (i n) -> p i n", i=2) for full in (g_sum, parts[:, 2, :])]
            for j in range(2):
                ins = V.tensor_copy(Grow[:, 0, j, :, 1:1 + H], rows[j])
            link(ins)
            for j in range(2):
                ins = V.tensor_tensor(Grow[:, 1, j, :, 1:1 + H], rows[j], Grow[:, 0, j, :, 1:1 + H], ALU.subtract)
            link(ins)
            for to, of in ((0, 2), (H + 1, H - 1), (H + 2, H - 2), (H + 3, 3)):
                for t in range(2):
                    V.tensor_copy(Grow[:, t, :, :, to:to + 1], Grow[:, t, :, :, of:of + 1])
            V.tensor_scalar(neg_mid[0:1, :, :], Grow[0:1, :, 1, 1, 1:1 + EW], -1.0, None, ALU.mult)\
                .then_inc(S["g_ready"], 1)
            first_stats(range(3, C // 4))

            def pair_stats(b, p):
                for k in range(2):
                    dve.wait_ge(st_in[k], (b - 1) * (16 * NPAIR) + 16 * p + 16)
                    V.bn_stats(bst1[:, bass.ds(2 * p + k, 1), :].rearrange("p c s -> p (c s)"), stat_in[:, k, :])\
                        .then_inc(S["st1_done"], 1)

            def link1(ins, b, n):
                ins.then_inc(S["link1"], 1)
                dve.wait_ge(S["link1"], b * LINKS1 + n)

            mean, var, w0, w1 = (gn1[:, n, :] for n in range(4))

            def spread1(b):
                dve.wait_ge(S["st1_done"], (b + 1) * C + PRIME["st1_done"])
                V.memset(gn1[:, 2:4, :], 0.0)
                for g in range(NPAIR):
                    ins = V.bn_aggr(mv1[:, g, :], bst1[:, 2 * g:2 * g + 2, :].rearrange("p c s -> p (c s)"))
                ins.then_inc(S["st1_v"], 1)

            def mean1(b):
                dve.wait_ge(S["st1_p"], b * 2 + 1)
                link1(V.tensor_copy(gn1[:, 0:2, :], sums1.rearrange("p (g s) -> p s g", s=2)), b, 1)
                link1(V.tensor_tensor(w0, mv1[:, :, 0], mean, ALU.subtract), b, 2)
                V.tensor_tensor(w0, w0, w0, ALU.mult).then_inc(S["st1_v"], 1)

            def scale1(b):
                dve.wait_ge(S["st1_p"], b * 2 + 2)
                dve.wait_ge(S["st1_v"], b * 3 + 2)
                V.scalar_tensor_tensor(var, sums1_sq, EPS, var, ALU.add, ALU.add)\
                    .then_inc(S["st1_v"], 1)
                dve.wait_ge(S["st1_a"], b + 1)
                dve.wait_ge(S["st1_v"], b * 3 + 3)
                link1(V.reciprocal(w0, w1), b, 3)
                link1(V.tensor_tensor(w0, w0, var, ALU.mult), b, 4)
                link1(V.tensor_tensor(w0, w0, w1, ALU.add), b, 5)
                link1(V.tensor_scalar(w0, w0, 0.5, None, ALU.mult), b, 6)
                link1(V.reciprocal(w0, w0), b, 7)
                link1(V.tensor_scalar(gn1[:, 4, :], w0, X_SCALE, None, ALU.mult), b, 8)
                link1(V.tensor_tensor(w0, mean, gn1[:, 4, :], ALU.mult), b, 9)
                V.tensor_scalar(gn1[:, 5, :], w0, -1.0, None, ALU.mult).then_inc(S["link1"], 1)

            spread1(0)
            mean1(0)
            scale1(0)

            def link2(ins, b, n):
                ins.then_inc(S["link2"], 1)
                dve.wait_ge(S["link2"], b * LINKS2 + n)

            def fold_pair(hf, g, k):
                wait(dve, "raw_lo", hf.pairs + g - 1)
                for c in range(2):
                    dve.wait_ge(S["norm_done"], 2 * hf.pairs + 2 * g + (c + 1))
                    a = raw[:, k, c]
                    V.tensor_tensor(fold[:, k, 0, c, :, 1:P], a[:, :, 1:P], a[:, :, W - 1:P:-1], ALU.add)
                    V.tensor_tensor(fold[:, k, 1, c, :, 1:P], a[:, :, 1:P], a[:, :, W - 1:P:-1], ALU.subtract)
                a = raw[:, k].rearrange("p c k w -> p (c k) w")
                e = fold[:, k].rearrange("p f c k w -> p f (c k) w")
                V.tensor_copy(e[:, :, :, 0].rearrange("p f n -> p n f"), a[:, :, 0:P + 1:P]).then_inc(S["raw_n"], 1)

            def ahead(hf, k):
                if hf and k in (0, 1, 3):
                    fold_pair(hf, k - k // 3, (0, 1, None, 0)[k])

            def normalise_x1(cb, e):
                dve.wait_ge(S["xc_in"], (cb * HALF + e + 1) * 16)
                V.tensor_scalar(x1t[:, :, 1:1 + W], x1t[:, :, 1:1 + W], gn2[:, 11:12], gn2[:, 12:13],
                                ALU.mult, ALU.add).then_inc(S["xc_pad"], 1)
                dve.wait_ge(S["xc_pad"], cb * HALF + e + 1)
                V.tensor_copy(x1t[:, :, 0:1], x1t[:, :, 2:3])
                V.tensor_copy(x1t[:, :, W + 1:W + 2], x1t[:, :, W - 1:W])
                V.tensor_copy(x1t[:, :, W + 2:W + 3], x1t[:, :, W - 2:W - 1])
                V.tensor_copy(x1t[:, :, W + 3:W + 4], x1t[:, :, 3:4]).then_inc(S["xc_n"], 1)

            def spread2(b):
                dve.wait_ge(S["st2_done"], (b + 1) * NBLK)
                link2(V.tensor_copy(bst2[0:C, 0, :], bst2[0:C, NBLK - 1, :]), b, 1)
                V.memset(gn2[:, 4:8], 0.0)
                V.bn_aggr(gn2[:, 0:2], bst2[:, 0:NBLK - 1, :].rearrange("p j s -> p (j s)")).then_inc(S["gn2_v"], 1)

            def mean2(b):
                dve.wait_ge(S["gn2_p"], b * 3 + 1)
                link2(V.tensor_copy(gn2[:, 2:4], sums2[:, 0:2]), b, 2)
                link2(V.tensor_tensor(gn2[:, 6:7], gn2[:, 0:1], gn2[:, 2:3], ALU.subtract), b, 3)
                V.tensor_tensor(gn2[:, 7:8], gn2[:, 6:7], gn2[:, 6:7], ALU.mult).then_inc(S["gn2_v"], 1)

            def var2(b):
                dve.wait_ge(S["gn2_p"], b * 3 + 2)
                dve.wait_ge(S["gn2_v"], b * 4 + 2)
                V.scalar_tensor_tensor(gn2[:, 4:5], sums2[:, 2:3], EPS, gn2[:, 3:4], ALU.add, ALU.add)\
                    .then_inc(S["gn2_v"], 1)

            def scale2(b):
                dve.wait_ge(S["gn2_a"], b + 1)
                dve.wait_ge(S["gn2_v"], b * 4 + 3)
                link2(V.reciprocal(gn2[:, 6:7], gn2[:, 5:6]), b, 4)
                link2(V.tensor_tensor(gn2[:, 6:7], gn2[:, 6:7], gn2[:, 4:5], ALU.mult), b, 5)
                link2(V.tensor_tensor(gn2[:, 6:7], gn2[:, 6:7], gn2[:, 5:6], ALU.add), b, 6)
                link2(V.tensor_scalar(gn2[:, 10:11], gn2[:, 6:7], 0.5, None, ALU.mult), b, 7)
                V.tensor_tensor(wmax[:, 1:2], wmax[:, 0:1], gn2[:, 10:11], ALU.add).then_inc(S["gn2_v"], 1)
                link2(V.reciprocal(gn2[:, 7:8], gn2[:, 10:11]), b, 8)
                link2(V.tensor_scalar(gn2[:, 11:12], gn2[:, 7:8], X_SCALE, None, ALU.mult), b, 9)
                link2(V.scalar_tensor_tensor(gn2[:, 12:13], gn2[:, 2:3], -1.0, gn2[:, 11:12], ALU.mult, ALU.mult), b, 10)
                V.scalar_tensor_tensor(convw_raw[:, :, 3, :], tapm[:, :, :], gn2[:, 10:11], middle[:, :, :],
                                       ALU.mult, ALU.add).then_inc(S["link2"], 1)

            def factor2(b):
                dve.wait_ge(S["gn2_p"], b * 3 + 3)
                link2(V.tensor_scalar(gn2[:, 13:14].bitcast(I32), sums2[:, 3:4].bitcast(I32), 0x7F800000, None,
                                      ALU.bitwise_and), b, 12)
                V.tensor_copy(gn2[:, 8:9], gn2[:, 2:3])
                V.tensor_scalar(gn2[:, 9:10], gn2[:, 13:14], 2.0 ** -14 / X_SCALE, None, ALU.mult)
                link2(V.reciprocal(gn2[:, 14:15], gn2[:, 13:14]), b, 13)
                V.tensor_scalar(gn2[:, 14:15], gn2[:, 14:15], 2.0 ** 14, None, ALU.mult).then_inc(S["link2"], 1)

            def weights(b):
                dve.wait_ge(S["link2"], (b + 1) * LINKS2)
                V.tensor_scalar(convw[:, 0], convw_raw[:, :, :, :], gn2[:, 14:15], None, ALU.mult)\
                    .then_inc(S["w_ready"], 1)
                wait(dve, "w_ready", b * 2 + 1)
                V.scalar_tensor_tensor(convw[:, 1], convw_raw[:, :, :, :], gn2[:, 14:15], convw[:, 0],
                                       ALU.mult, ALU.subtract).then_inc(S["w_ready"], 1)

            def half(hf):
                b = hf.b

                def product_lo(c, s):
                    dve.wait_ge(S["z_hi"], hf.chans + c + 1)
                    V.scalar_tensor_tensor(Z[:, 1, :, 0:hf.rows, bass.ds(c, 1)].rearrange("p k r c -> p k (r c)"),
                                           rows_of(s, hf.rows), 1.0 / G_SCALE,
                                           Z[:, 0, :, 0:hf.rows, bass.ds(c, 1)].rearrange("p k r c -> p k (r c)"),
                                           ALU.mult, ALU.subtract).then_inc(S["s1_free"], 1)

                def pair(g, k):
                    fold_pair(hf, g + AHEAD, (k + AHEAD) % 2)
                    for e in range(2):
                        product_lo(2 * g + e, (2 * k + e) % 4)

                parts = {1: mean2, 3: var2, 4: scale2, 5: factor2} if hf.h == 0 and hf.conv else {}
                if parts:
                    spread2(b - 1)
                peeled = 7 if parts else 1
                for g in range(peeled):
                    pair(g, g)
                    if g in parts:
                        parts[g](b - 1)
                with dve.Fori(0, (NPAIR - AHEAD - peeled) // 2) as i:
                    for k in range(2):
                        pair(2 * i + (k + peeled), k + peeled)
                if parts:
                    normalise_x1(b - 1, 0)
                    weights(b - 1)
                for c in range(C - 2 * AHEAD, C):
                    product_lo(c, c % 4)

                def step(u, s, pair):
                    if hf.has(u):
                        n, k = hf.blocks(u), 2 * (s % 2)
                        dve.wait_ge(S["odd_done"], hf.first + u + 1)
                        ev = psum[:, k:k + n, 0:2 * EW].rearrange("p j (i w) -> p j i w", i=2)[:, :, :, 1:EW - 1]
                        od = odd[:, s % 2, 0:n, :].rearrange("p j (i w) -> p j i w", i=2)
                        V.tensor_tensor(trf[:, s, 0:n, :, 1:EW - 1], ev, od, ALU.add)
                        V.tensor_tensor(trf[:, s, 0:n, :, W - 1:EW - 1:-1], ev, od, ALU.subtract).then_inc(S["y_free"], 1)
                    if hf.has(u - 1):
                        v, t, m = u - 1, (s + 3) % 4, hf.blocks(u - 1)
                        d = sq[:, t % 2, 0, 0:m]
                        dve.wait_ge(S["d_done"], hf.first + v + 1)
                        V.reciprocal(d, d).then_inc(S["rec_done"], 1)
                    if hf.has(u - 2):
                        v, t, m = u - 2, (s + 2) % 4, hf.blocks(u - 2)
                        dve.wait_ge(S["sgn_done"], hf.first + v + 1)
                        V.scalar_tensor_tensor(ang[:, t, 0:m], ang[:, t, 0:m], float(np.pi / 4), trf[:, t, 0:m, 1, :],
                                               ALU.subtract, ALU.mult).then_inc(S["ang_done"], 1)
                    if hf.has(u - 3):
                        v, t, m = u - 3, (s + 1) % 4, hf.blocks(u - 3)
                        per = 9 if t == 0 else 8
                        dve.wait_ge(S["mix_mm"], hf.first + v + 1)
                        if isinstance(v, int):
                            dve.wait_ge(res_in[t], b * (64 * per) + 256 * hf.h + 64 * (v // 4 + 1))
                        else:
                            dve.wait_ge(res_in[t], b * (64 * per) + 256 * hf.h + 16 * v + (64 - 16 * t))
                        V.tensor_tensor(res[:, t, 0:m, :], psum[:, 4 + t % 2, 0:256 * m].rearrange("p (j w) -> p j w", j=m),
                                        res[:, t, 0:m, :], ALU.add).then_inc(S["x1_done"], 1)
                        dve.wait_ge(S["x1_done"], hf.first + v + 1)
                        for e in range(m):
                            V.bn_stats(bst2[:, bass.ds(2 * v + (e + 2 * HALF * hf.h), 1), :].rearrange("p c s -> p (c s)"),
                                       res[:, t, e, :]).then_inc(S["st2_done"], 1)
                    if hf.stat(u) is not None:
                        pair_stats(b + 1, u - 3)
                    e = hf.next_chunk(pair)
                    if e is not None:
                        normalise_x1(b - 1, e)

                def start(k):
                    if hf.h == 1 and hf.stats:
                        (spread1, mean1, scale1)[k](b + 1)

                walk(dve, step, hf.n, start, lambda k: ahead(after(hf), k))

            def last():
                for part in (spread2, mean2, var2, scale2, factor2):
                    part(B - 1)
                normalise_x1(B - 1, 0)
                weights(B - 1)
                with dve.Fori(1, HALF) as e:
                    normalise_x1(B - 1, e)

            for k in range(4):
                ahead(Half(0, 0, False, True), k)
            batches(dve, half, last)

        @block.tensor
        def _(pe):
            T = nc.tensor
            pe.wait_ge(S["g_ready"], 1)
            for j, r, tables in ((0, 0, (0,)), (1, 0, (1,)), (2, 1, (0, 1))):
                terms = [(t, k) for t in tables for k in range(2)]
                for t, k in terms:
                    ins = T.matmul(psum[:, j, :], dft[:, t, k, P * r:P * r + P], kern[:, t, k, :],
                                   start=(t, k) == terms[0], stop=(t, k) == terms[-1])
            ins.then_inc(S["setup_mm"], 1)

            def sum1(b, n):
                pe.wait_ge(S["st1_v"], b * 3 + (n + 1))
                if n == 0:
                    T.matmul(sums1, ones[:, :], mv1[:, :, :].rearrange("p g s -> p (g s)"), start=True, stop=True)\
                        .then_inc(S["st1_p"], 1)
                else:
                    T.matmul(sums1_sq, ones[:, :], gn1[:, 2, :], start=True, stop=True).then_inc(S["st1_p"], 1)

            def sum2(cb, n):
                pe.wait_ge(S["gn2_v"], cb * 4 + (1, 2, 4)[n])
                to, by, of = ((sums2[:, 0:2], quadm, gn2[:, 0:2]), (sums2[:, 2:3], quadm, gn2[:, 7:8]),
                              (sums2[:, 3:4], ones, wmax[:, 1:2]))[n]
                T.matmul(to, by[:, :], of, start=True, stop=True).then_inc(S["gn2_p"], 1)

            def sum2_read(cb, n):
                name, value = (("link2", cb * LINKS2 + 2), ("gn2_v", cb * 4 + 3), ("link2", cb * LINKS2 + 12))[n]
                pe.wait_ge(S[name], value)

            def conv_pair(cb, p, chunk, k, j):
                wait(pe, "cv_free", cb * NOUT + p - 1)
                wait(pe, "w_ready", cb * 2 + 2)
                wait(pe, "xc_lo", cb * HALF + chunk + 1)
                n = 0
                for kb in range(2):
                    for kx in range(KT):
                        for xt, wt in ((0, 0), (1, 0), (0, 1)):
                            ins = T.matmul(psum[:, 6 + j, :], convw[:, wt, kb, kx, :],
                                           conv_in[:, k, xt, 2 * j + kb:2 * j + kb + 2, 4 - kx:4 - kx + W],
                                           start=n == 0, stop=n == 29)
                            n += 1
                ins.then_inc(S["cv_mm"], 1)

            def half(hf):
                b, R = hf.b, hf.rows
                first_row = ROWS[0] * hf.h

                def channel(c, k, e, sums=None):
                    s = (2 * k + e) % 4
                    wait(pe, "s1_free", hf.chans + c - 3)
                    first = not isinstance(hf.first, int) or hf.first > 0
                    if first and s == 0:
                        wait(pe, "y_free", hf.first)
                    if first and s == 2:
                        pe.wait_ge(S["x1_done"], hf.first)
                    if s == 3 and hf.conv:
                        wait(pe, "cv_free", (b - 1) * NOUT + HALF * hf.h)
                    if sums is not None:
                        sum2(b - 1, sums)
                    for f in range(2):
                        n = 0
                        if f == 1 and sums is not None:
                            sum2_read(b - 1, sums)
                        for kb in range(NB):
                            for xt, gt in ((0, 0), (0, 1), (1, 0)):
                                ins = T.matmul(psum[:, 2 * s + f, :].rearrange("p (i r) -> p i r", i=2)[:, :, 0:R],
                                               split[:, k, xt, f, e, kb, :],
                                               Grow[:, gt, kb, :, first_row:first_row + R], start=n == 0, stop=n == 5)
                                n += 1
                    ins.then_inc(S["s1_mm"], 1)

                pe.wait_ge(S["g_ready"], 2)
                def rows_pair(g, k, sums=None):
                    wait(pe, "raw_lo", hf.pairs + g + 1)
                    for e in range(2):
                        channel(2 * g + e, k, e, None if e else sums)

                turns = 2 if hf.h == 0 and hf.conv else 0
                for g in range(4 * turns):
                    rows_pair(g, g % 4, {3: 0, 5: 1, 7: 2}.get(g))
                with pe.Fori(turns, NPAIR // 4) as i:
                    for k in range(4):
                        rows_pair(4 * i + k, k)

                def transform(u, s, n):
                    if isinstance(u, int) and u == 0:
                        pe.wait_ge(S["gcol_ready"], 1)
                        pe.wait_ge(S["mid_in"], 192)
                        pe.wait_ge(S["zmid_in"], (b * 2 + hf.h + 1) * 96)
                    wait(pe, "y_free", hf.first + u - 1)
                    for j in range(n):
                        cols = bass.ds((2 * u + j) * P, P)
                        for f, base, w, at in ((0, 0, EW, 0), (1, 3 * EW, OW, 2 * EW)):
                            dst = psum[:, 2 * (s % 2) + j, at:at + 2 * w]
                            m = 0
                            for ri in range(2):
                                for zt, gt in ((0, 0), (0, 1), (1, 0)):
                                    c0 = base + (1 - ri) * w
                                    ins = T.matmul(dst, Zflat[:, 4 * zt + 2 * f + ri, cols], Gcol[:, gt, c0:c0 + 2 * w],
                                                   start=m == 0, stop=f == 1 and m == 5)
                                    m += 1
                            if f == 0:
                                ins = T.matmul(dst, Zmid[:, cols], Gmid[:, :], start=False, stop=True)
                    ins.then_inc(S["s2_mm"], 1)

                def mix(u, s, n):
                    pe.wait_ge(S["ang_done"], hf.first + u + 1)
                    dst = psum[:, 4 + s % 2, 0:256 * n]
                    T.matmul(dst, mixw[:, 0, :], mag[:, s, 0:n].rearrange("p j w -> p (j w)"), start=True, stop=False)
                    T.matmul(dst, mixw[:, 1, :], ang[:, s, 0:n].rearrange("p j w -> p (j w)"),
                             start=False, stop=True).then_inc(S["mix_mm"], 1)

                def step(u, s, pair):
                    if isinstance(u, int) and u == 0:
                        wait(pe, "s1_free", hf.chans + C)
                    if pair is not None and hf.conv:
                        conv_pair(b - 1, pair.p + HALF * hf.h, pair.c + HALF // 2 * hf.h, pair.k, pair.j)
                    if hf.has(u):
                        transform(u, s, hf.blocks(u))
                    if hf.has(u - 3):
                        mix(u - 3, (s + 1) % 4, hf.blocks(u - 3))

                def start(k):
                    if k and hf.h == 1 and hf.stats:
                        sum1(b + 1, k - 1)

                walk(pe, step, hf.n, start, lambda k: None)

            def last():
                wait(pe, "cv_free", (B - 1) * NOUT)
                for n in range(3):
                    sum2(B - 1, n)
                with pe.Fori(0, HALF // 2) as i:
                    for k in range(2):
                        for j in range(2):
                            conv_pair(B - 1, 4 * i + (2 * k + j), 2 * i + k, k, j)

            for n in range(2):
                sum1(0, n)
            batches(pe, half, last)


def kernel(**inputs):
    import concourse.bacc as bacc
    from concourse.bass_utils import run_bass_kernel_spmd

    f32 = mybir.dt.float32
    x = np.ascontiguousarray(inputs["x"])
    B, C, H, W = x.shape
    Q = P // C
    w0 = np.asarray(inputs["L0_conv_w"])
    w1 = np.asarray(inputs["L1_conv_weight"])
    KT = w1.shape[-1]

    mix_w = np.zeros((P, 2, P), w0.dtype)
    for q in range(Q):
        for part in range(2):
            mix_w[q * C:(q + 1) * C, part, q * C:(q + 1) * C] = w0[:, part * C:(part + 1) * C].T
    conv_w = np.zeros((P, 2, KT, P), w1.dtype)
    tap = np.zeros((P, 2, P), np.float32)
    for q in range(Q):
        for ky in range(KT):
            kb, qi = divmod(q + 4 - ky, Q)
            for kx in range(KT):
                conv_w[qi * C:(qi + 1) * C, kb, kx, q * C:(q + 1) * C] = w1[:, :, ky, kx].T
        kb, qi = divmod(q + 1, Q)
        tap[qi * C:(qi + 1) * C, kb, q * C:(q + 1) * C] = np.eye(C, dtype=np.float32)
    group = (np.arange(P) % C) // 2
    quad_mean = ((group[:, None] == group[None, :]) / (2.0 * Q)).astype(np.float32)
    n = np.arange(W)
    pos = np.minimum(n, W - n).astype(np.float64) ** 2
    frq = (n - W // 2).astype(np.float64) ** 2
    grid_sq = np.concatenate([pos.reshape(2, P).T, frq.reshape(2, P).T, np.tile(pos, (P, 1))], axis=1).astype(np.float32)
    turn = 2 * np.pi * (np.outer(n, n) % W) / W
    arrays = {
        "x": x, "alpha": np.asarray(inputs["L0_conv_alpha"]).reshape(1, 1), "grid_sq": grid_sq,
        "dft_cos": np.cos(turn).astype(np.float32), "dft_sin": np.sin(turn).astype(np.float32),
        "mix_w": mix_w, "conv_w": conv_w, "tap": tap, "quad_mean": quad_mean,
    }
    nc = bacc.Bacc("TRN2", target_bir_lowering=False, num_devices=1)
    args = [nc.dram_tensor(k, a.shape, f32, kind="ExternalInput").ap() for k, a in arrays.items()]
    args.append(nc.dram_tensor("out", x.shape, f32, kind="ExternalOutput").ap())
    args.append(nc.dram_tensor("x1_dram", (B, P, H // Q + 1, W), f32, kind="Internal").ap())
    frft_conv_kernel(nc, *args)
    r = run_bass_kernel_spmd(nc, [arrays], core_ids=[0])
    return r.results[0]["out"]
```

```python
from contextlib import ExitStack

import numpy as np

import concourse.bass as bass
from concourse import mybir


P = 128
F32 = mybir.dt.float32
F16 = mybir.dt.float16
I32 = mybir.dt.int32
ALU = mybir.AluOpType
ACT = mybir.ActivationFunctionType
AX_X = mybir.AxisListType.X

PI = float(np.float32(np.pi))
PI_LOW = float(np.pi - np.float64(np.float32(np.pi)))
HALF_PI = float(np.float32(np.pi / 2))
HALF_PI_LOW = float(np.pi / 2 - np.float64(np.float32(np.pi / 2)))
TWO_PI_A = 6.28125
TWO_PI_B = float(np.float32(2 * np.pi - TWO_PI_A))
TWO_PI_C = float(np.float32(2 * np.pi - TWO_PI_A - np.float64(np.float32(2 * np.pi - TWO_PI_A))))
ROUND = 12582912.0
X_SCALE = 64.0
G_SCALE = 4096.0
W_SCALE = 128.0
EPS = 1e-5


def frft_conv_kernel(nc, x, alpha, grid_sq, dft_cos, dft_sin, mix_w, conv_w, tap, quad_mean, out, x1_dram):
    B, C, H, W = x.shape
    Q = P // C
    NPAIR = C // 2
    NB = H // P
    EW, OW = W // 2 + 1, W // 2 - 1
    NBLK = H // Q + 1
    NUNIT = NBLK // 2 + 1
    HALF = NUNIT // 2
    ROWS = (HALF * 2 * Q, HALF * 2 * Q + Q)
    RMAX = ROWS[1]
    EXT = H + 4
    WP = W + 4
    KT = 5
    NOUT = H // Q // 2
    AHEAD = 3
    LINKS1 = 10
    LINKS2 = 15
    CB = 5
    assert P == Q * C and NB == 2 and NBLK == 65 and NUNIT == 33 and NOUT == 2 * HALF

    with ExitStack() as ctx:
        def sb(name, shape, dt=F32):
            return ctx.enter_context(nc.sbuf_tensor(name, shape, dt))

        psum = ctx.enter_context(nc.psum_tensor("psum", [P, 8, 512], F32))

        arena = sb("arena", [P, 8 * RMAX * C // 2])
        Zflat = arena[:, :].bitcast(F16).rearrange("p (l n) -> p l n", l=8)
        Z = arena[:, :].bitcast(F16).rearrange("p (t k r c) -> p t k r c", t=2, k=4, c=C)
        dft = arena[:, 0:1024].rearrange("p (s k m) -> p s k m", s=2, k=2)
        kern = arena[:, 1024:3072].rearrange("p (s k n) -> p s k n", s=2, k=2)
        part_tmp = arena[:, 3072:6144].rearrange("p (i n) -> p i n", n=256)
        parts = arena[:, 6144:7680].rearrange("p (j n) -> p j n", j=3)
        g_sum = arena[:, 7680:8192]
        grid = arena[:, 8192:8712].rearrange("p (i n) -> p i n", i=2)

        Zmid = sb("Zmid", [P, RMAX * C], F16)
        Grow = sb("Grow", [P, 2, NB, 2, EXT], F16)
        Gcol = sb("Gcol", [P, 2, 3 * (EW + OW)], F16)
        Gmid = sb("Gmid", [P, 2 * EW], F16)
        neg_mid = sb("neg_mid", [1, 2, EW], F16)
        mixw = sb("mixw", [P, 2, P])
        convw = sb("convw", [P, 2, 3, KT, P], F16)
        tapm = sb("tapm", [P, 2, P])
        quadm = sb("quadm", [P, P])
        ones = sb("ones", [P, P])
        tiny = sb("tiny", [P, 1])
        raw = sb("raw", [P, 2, 2, NB, W])
        fold = sb("fold", [P, 2, 2, 2, NB, P])
        split = sb("split", [P, 4, 2, 2, 2, NB, P], F16)
        res = sb("res", [P, 4, 2, W])
        trf = sb("trf", [P, 4, 2, 2, W])
        odd = sb("odd", [P, 2, 2, 2 * OW])
        sq = sb("sq", [P, 2, 2, 2, W])
        convw_raw = sq[:, :].rearrange("p a b c w -> p (a b c w)")[:, 0:3 * KT * P]\
            .rearrange("p (s k m) -> p s k m", s=3, k=KT)
        mag = sb("mag", [P, 4, 2, W])
        ang = sb("ang", [P, 4, 2, W])
        stat_in = sb("stat_in", [P, 2, 2 * W])
        x1t = sb("x1t", [P, CB + 1, WP])
        x1t_more = arena[:, 0:(CB + 1) * WP].rearrange("p (j w) -> p j w", j=CB + 1)
        conv_in = sb("conv_in", [P, 2, 2, CB + 1, WP], F16)
        outs = sb("outs", [P, 2, 2, W])

        ang_s = sb("ang_s", [P, 3, 3])
        sc = sb("sc", [P, 16])
        bst1 = sb("bst1", [P, C, 6])
        mv1 = sb("mv1", [P, NPAIR, 2])
        gn1 = sb("gn1", [P, 6, NPAIR])
        bst2 = sb("bst2", [P, NBLK, 6])
        gn2 = sb("gn2", [P, 16])
        wmax = sb("wmax", [P, 3])

        names = """primed consts_in first_in0 first_in1 parts_done gcol_hi gcol_lo gcol_ready setup_p setup_v setup_a setup_mm g_ready mid_in link raw_in0 raw_in1 norm_own norm_done raw_n raw_hi raw_lo
            s1_mm s1_free z_hi zmid_in s2_mm y_free odd_done sq_done sum_done r_done d_done rec_done u_done at_done
            sgn_done ang_done mix_mm x1_done st2_done res_in0 res_in1 res_in2 res_in3 x1_out0 x1_out1 x1_out2 x1_out3
            st_in0 st_in1 st1_done st1_v st1_p st1_a gn2_v gn2_p gn2_a w_in w_ready link1 link2
            xc_in xc_more_in xc_pad xc_n xc_extra xc_dif xc_hi xc_lo cv_mm cv_part cv_free cv_out0 cv_out1""".split()
        S = {n: ctx.enter_context(nc.semaphore(n)) for n in names}
        raw_in = [S["raw_in0"], S["raw_in1"]]
        res_in = [S[f"res_in{i}"] for i in range(4)]
        x1_out = [S[f"x1_out{i}"] for i in range(4)]
        st_in = [S["st_in0"], S["st_in1"]]
        first_in = [S["first_in0"], S["first_in1"]]
        cv_out = [S["cv_out0"], S["cv_out1"]]

        x_rows = x.rearrange("b c (k p) w -> b p c k w", p=P)
        x_stat = x.rearrange("b c (p r) w -> b p c (r w)", p=P)

        sums1 = psum[:, 4, 192:192 + 2 * NPAIR]
        sums1_sq = psum[:, 4, 224:224 + NPAIR]
        sums2 = psum[:, 5, 240:244]
        def rows_of(s, n):
            return psum[:, 2 * s:2 * s + 2, :].rearrange("p j (i r) -> p (j i) r", i=2)[:, :, 0:n]

        PRIME = {"raw_n": 2, "raw_lo": 2, "s1_free": 4, "y_free": 2, "cv_free": 2, "cv_part": 2, "cv_out0": 64, "cv_out1": 64,
                 "st1_done": 2, "xc_lo": 1, "w_ready": 1, "x1_out0": 16, "x1_out1": 16, "x1_out2": 16, "x1_out3": 16}

        def wait(eng, name, n):
            eng.wait_ge(S[name], n + PRIME.get(name, 0))

        class Pair:

            def __init__(self, p, j, c, k):
                self.p, self.j, self.c, self.k = p, j, c, k

        def walk(eng, step, n, start, ahead):
            for u, pair in ((0, Pair(0, 0, 0, 0)), (1, None), (2, Pair(1, 1, 0, 0))):
                start(u)
                step(u, u, pair)
            with eng.Fori(0, 3) as i:
                for q in range(4):
                    step(4 * i + (q + 3), (q + 3) % 4,
                         Pair(4 * i + (q + 2), q % 2, 2 * i + (1 + q // 2), (1 + q // 2) % 2))
            for u in range(15, n + 3):
                ahead(u - 15)
                step(u, u % 4, {HALF - 1: Pair(HALF - 2, 0, HALF // 2 - 1, 1), HALF + 1: Pair(HALF - 1, 1, HALF // 2 - 1, 1)}.get(u))

        class Half:

            def __init__(self, b, h, conv, stats):
                self.b, self.h, self.conv, self.stats = b, h, conv, stats
                self.n = HALF + h
                self.first = b * NUNIT + HALF * h
                self.pairs = (b * 2 + h) * NPAIR
                self.chans = (b * 2 + h) * C
                self.rows = ROWS[h]

            def has(self, v):
                return not isinstance(v, int) or 0 <= v < self.n

            def blocks(self, v):
                return 1 if isinstance(v, int) and v == HALF else 2

            def next_chunk(self, pair, j):
                if pair is None or not self.conv or pair.j != j or (self.h and isinstance(pair.c, int) and pair.c == HALF // 2 - 1):
                    return None
                return pair.c + (HALF // 2 * self.h + 1)

            def ended(self, u, pair):
                if not self.conv:
                    return None
                if pair is not None and pair.j == 0 and not (isinstance(u, int) and u == 0):
                    return pair.c + (HALF // 2 * self.h - 1)
                return HALF // 2 * self.h + HALF // 2 - 1 if isinstance(u, int) and u == HALF + 2 else None

            def stat(self, u):
                p = u - 3
                if not self.stats or self.h or (isinstance(p, int) and not 0 <= p < HALF):
                    return None
                return p

        def batches(eng, half, last_conv):
            def batch(b, conv, stats):
                half(Half(b, 0, conv, stats))
                half(Half(b, 1, conv, stats))

            batch(0, False, True)
            with eng.Fori(1, B - 1) as b:
                batch(b, True, True)
            batch(B - 1, True, False)
            last_conv()

        def after(hf):
            if hf.h == 0:
                return Half(hf.b, 1, hf.conv, hf.stats)
            return Half(hf.b + 1, 0, True, True) if hf.stats else None

        GCOL = ((0, 0, EW), (3 * EW, 1, OW))

        def gcol_part(j):
            base, first, n = GCOL[j]
            part = parts[:, j, :].rearrange("p (i n) -> p i n", i=2)[:, :, first:first + n]
            return (part, *(Gcol[:, t, base + n:base + 3 * n].rearrange("p (i n) -> p i n", i=2) for t in range(2)))

        def minus_im(j):
            base, _, n = GCOL[j]
            return [Gcol[:, t, base:base + n] for t in range(2)]

        def four_channels(k):
            return trf[:, 2 * k:2 * k + 2].rearrange("p s b i w -> p (s b) (i w)")

        block = ctx.enter_context(nc.Block())

        @block.sync
        def _(sp):
            sp.dma_start(grid[:, 0, :], grid_sq).then_inc(S["consts_in"], 16)
            sp.dma_start(sc[:, 0:1], alpha.to_broadcast([P, 1])).then_inc(S["consts_in"], 16)
            sp.dma_start(dft[:, 0, :, :], dft_cos.rearrange("(k p) m -> p k m", p=P)).then_inc(S["consts_in"], 16)
            sp.dma_start(dft[:, 1, :, :], dft_sin.rearrange("(k p) m -> p k m", p=P)).then_inc(S["consts_in"], 16)
            sp.dma_start(mixw[:, :, :], mix_w).then_inc(S["consts_in"], 16)
            sp.dma_start(tapm[:, :, :], tap).then_inc(S["consts_in"], 16)
            sp.dma_start(quadm[:, :], quad_mean).then_inc(S["consts_in"], 16)
            sp.dma_start(convw_raw[:, 0:2], conv_w).then_inc(S["w_in"], 16)

            def load_stats(b, p):
                wait(sp, "st1_done", b * C + 2 * p)
                for k in range(2):
                    sp.dma_start(stat_in[:, k, :], x_stat[bass.ds(b, 1), :, bass.ds(2 * p + k, 1), :]
                                 .rearrange("b p c n -> (b p) (c n)")).then_inc(st_in[k], 16)

            def load_raw(hf, g, k, free=False):
                if not free:
                    wait(sp, "raw_n", hf.pairs + g - 1)
                sp.dma_start(raw[:, k, :, :, :], x_rows[bass.ds(hf.b, 1), :, bass.ds(2 * g, 2), :, :]
                             .rearrange("b p c k w -> (b p) c k w")).then_inc(raw_in[k], 16)

            sp.wait_ge(S["primed"], 1)
            for g in range(C // 4):
                if g >= 2:
                    wait(sp, "st1_done", 4 * (g - 1))
                sp.dma_start(four_channels(g % 2), x_stat[0, :, 4 * g:4 * g + 4, :]).then_inc(first_in[g % 2], 16)

            sp.wait_ge(S["g_ready"], 2)
            sp.wait_ge(S["setup_p"], 1)
            for r, (t, im) in enumerate(((0, 0), (0, 0), (1, 0), (0, 1), (0, 1), (1, 1))):
                first = neg_mid[0:1, t, :] if im else Grow[0:1, t, 1, 0, 1:1 + EW]
                second = Grow[0:1, t, 1, 0 if im else 1, 1:1 + EW]
                sp.dma_start(Gmid[r:r + 1, 0:EW], first).then_inc(S["mid_in"], 16)
                sp.dma_start(Gmid[r:r + 1, EW:2 * EW], second).then_inc(S["mid_in"], 16)

            def load_res(hf, u, s):
                b, h = hf.b, hf.h
                per = 9 if s == 0 else 8
                wait(sp, f"x1_out{s}", b * (16 * per) + 64 * h + 4 * (u - s))
                for q in range(Q):
                    row = 8 * u + (q - 1 + 8 * HALF * h)
                    if isinstance(u, int) and u == 0 and h == 0 and q == 0:
                        rows = x[bass.ds(b, 1), :, 1:4:2, :]
                    elif isinstance(u, int) and u == HALF:
                        r = [H - 1, H - 2, H - 3, 2][q]
                        rows = x[bass.ds(b, 1), :, r:r + 1, :]
                    else:
                        rows = x[bass.ds(b, 1), :, bass.ds(row, 2, step=4), :]
                    sp.dma_start(res[C * q:C * q + C, s, 0:hf.blocks(u), :], rows.rearrange("b c r w -> (b c) r w"))\
                      .then_inc(res_in[s], 16)

            def load_chunk(cb, e, buf=x1t, ring=1):
                wait(sp, "xc_lo", cb * HALF + e + (1 - ring))
                sp.dma_start(buf[:, 0:CB, 1:1 + W], x1_dram[bass.ds(cb, 1), :, bass.ds(4 * e, CB), :]
                             .rearrange("b p j w -> (b p) j w")).then_inc(S["xc_in" if buf is x1t else "xc_more_in"], 16)

            def store_out(cb, c, k):
                wait(sp, "cv_free", cb * NOUT + 2 * c + (k + 1))
                for q in range(Q):
                    sp.dma_start(out[bass.ds(cb, 1), :, bass.ds(16 * c + (4 * k + q), 2, step=8), :]
                                 .rearrange("b c r w -> (b c) r w"), outs[C * q:C * q + C, k, :, :])\
                      .then_inc(cv_out[k], 16)

            def load_weights(cb):
                sp.wait_ge(S["u_done"], (cb + 1) * NUNIT)
                sp.dma_start(convw_raw[:, 0:2], conv_w).then_inc(S["w_in"], 16)

            def start_conv(cb):
                for s in range(4):
                    wait(sp, f"x1_out{s}", (cb + 1) * (16 * (9 if s == 0 else 8)))
                load_chunk(cb, 0)

            def pre(hf):
                load_raw(hf, 1, 1)
                load_raw(hf, 0, 0, free=True)

            def ahead(hf, k):
                if hf and k in (1, 2):
                    load_raw(hf, k + 1, k - 1)

            def half(hf):
                b = hf.b
                if hf.h == 0 and hf.conv:
                    load_weights(b - 1)
                with sp.Fori(0, NPAIR // 2 - 2) as i:
                    for k in range(2):
                        load_raw(hf, 2 * i + (k + 4), k)
                if hf.h == 0 and hf.conv:
                    start_conv(b - 1)
                load_res(hf, 0, 0)
                sp.wait_ge(S["s1_free"], hf.chans + C + 4)
                for r, (t, ri) in enumerate(((0, 0), (1, 0), (0, 0), (0, 1), (1, 1), (0, 1))):
                    sp.dma_start(Zmid[r:r + 1, 0:hf.rows * C], Zflat[0:1, 4 * t + 2 + ri, 0:hf.rows * C])\
                      .then_inc(S["zmid_in"], 16)

                def step(u, s, pair):
                    e = hf.next_chunk(pair, 0)
                    if e is not None:
                        load_chunk(b - 1, e)
                    if hf.stat(u) is not None:
                        load_stats(b + 1, u - 3)
                    if hf.has(u - 1) and not (isinstance(u, int) and u == 1):
                        load_res(hf, u - 1, (s + 3) % 4)
                    if hf.has(u - 3):
                        v, t, m = u - 3, (s + 1) % 4, hf.blocks(u - 3)
                        sp.wait_ge(S["x1_done"], hf.first + v + 1)
                        sp.dma_start(x1_dram[bass.ds(b, 1), :, bass.ds(2 * v + 2 * HALF * hf.h, m), :]
                                     .rearrange("b p j w -> (b p) j w"), res[:, t, 0:m, :]).then_inc(x1_out[t], 16)
                    c = hf.ended(u, pair)
                    if c is not None:
                        for k in range(2):
                            store_out(b - 1, c, k)
                    if isinstance(u, int) and u == 2 and after(hf):
                        pre(after(hf))

                walk(sp, step, hf.n, lambda k: None, lambda k: ahead(after(hf), k))

            def last():
                load_weights(B - 1)
                start_conv(B - 1)
                load_chunk(B - 1, 1, x1t_more, 2)
                with sp.Fori(0, HALF // 2 - 1) as i:
                    for e, buf in enumerate((x1t, x1t_more)):
                        load_chunk(B - 1, 2 * i + (e + 2), buf, 2)
                        for k in range(2):
                            store_out(B - 1, 2 * i + e, k)
                for e in (HALF - 2, HALF - 1):
                    for k in range(2):
                        store_out(B - 1, e, k)
                for k in range(2):
                    wait(sp, f"cv_out{k}", B * HALF * 64)

            pre(Half(0, 0, False, True))
            for k in range(4):
                ahead(Half(0, 0, False, True), k)
            batches(sp, half, last)

        @block.gpsimd
        def _(pool):
            for name, n in PRIME.items():
                pool.sem_inc(S[name], n)
            pool.sem_inc(S["primed"], 1)
            nc.gpsimd.memset(Zmid[:, :], 0.0)
            nc.gpsimd.memset(Gmid[:, :], 0.0).then_inc(S["setup_p"], 1)

            pool.wait_ge(S["gcol_hi"], 1)
            for j in range(2):
                part, hi, lo = gcol_part(j)
                ins = nc.gpsimd.tensor_tensor(lo, part, hi, ALU.subtract)
            ins.then_inc(S["gcol_lo"], 1)

            def pair_lo(hf, g, k):
                pool.wait_ge(S["raw_hi"], hf.pairs + g + 1)
                nc.gpsimd.tensor_tensor(split[:, k, 1], fold[:, k % 2], split[:, k, 0], ALU.subtract)\
                    .then_inc(S["raw_lo"], 1)

            def ahead(hf, k):
                if hf and k < 2:
                    pair_lo(hf, k, k)

            def chunk_differences(cb, e, buf=x1t):
                pool.wait_ge(S["xc_n"], cb * HALF + e + 1)
                nc.gpsimd.tensor_tensor(buf[:, 5, :], buf[:, 2, :], buf[:, 3, :], ALU.subtract)\
                    .then_inc(S["xc_extra"], 1)
                nc.gpsimd.tensor_tensor(buf[:, 0, :], buf[:, 0, :], buf[:, 1, :], ALU.subtract)
                pool.wait_ge(S["xc_extra"], cb * HALF + e + 1)
                nc.gpsimd.tensor_tensor(buf[:, 2:5:2, :], buf[:, 2:5:2, :], buf[:, 1:4:2, :], ALU.subtract)\
                    .then_inc(S["xc_dif"], 1)

            def chunk_lo(cb, e, k, buf=x1t):
                pool.wait_ge(S["xc_hi"], cb * HALF + e + 1)
                nc.gpsimd.tensor_tensor(conv_in[:, k, 1], buf[:, :, :], conv_in[:, k, 0], ALU.subtract)\
                    .then_inc(S["xc_lo"], 1)

            def half(hf):
                pair_lo(hf, 2, 2)
                with pool.Fori(0, NPAIR // 4 - 1) as i:
                    for k in range(4):
                        pair_lo(hf, 4 * i + (k + AHEAD), (k + AHEAD) % 4)
                pair_lo(hf, NPAIR - 1, 3)
                if hf.h == 0 and hf.conv:
                    chunk_differences(hf.b - 1, 0)
                    chunk_lo(hf.b - 1, 0, 0)

                def step(u, s, pair):
                    if hf.has(u):
                        n = hf.blocks(u)
                        pool.wait_ge(S["sq_done"], hf.first + u + 1)
                        nc.gpsimd.tensor_tensor(sq[:, s % 2, 0, 0:n], sq[:, s % 2, 0, 0:n], sq[:, s % 2, 1, 0:n], ALU.add)\
                            .then_inc(S["sum_done"], 1)
                    if hf.has(u - 1):
                        v, t, m = u - 1, (s + 3) % 4, hf.blocks(u - 1)
                        pool.wait_ge(S["rec_done"], hf.first + v + 1)
                        nc.gpsimd.tensor_tensor(ang[:, t, 0:m], trf[:, t, 0:m, 0, :], sq[:, t % 2, 0, 0:m], ALU.mult)\
                            .then_inc(S["u_done"], 1)
                    if hf.has(u):
                        pool.wait_ge(S["r_done"], hf.first + u + 1)
                        nc.gpsimd.tensor_tensor(sq[:, s % 2, 0, 0:n], sq[:, s % 2, 1, 0:n], mag[:, s, 0:n], ALU.add)\
                            .then_inc(S["d_done"], 1)
                    e = hf.next_chunk(pair, 0)
                    if e is not None:
                        chunk_differences(hf.b - 1, e)
                    e = hf.next_chunk(pair, 1)
                    if e is not None:
                        chunk_lo(hf.b - 1, e, 1 - pair.k)

                walk(pool, step, hf.n, lambda k: None, lambda k: ahead(after(hf), k))

            def last():
                chunk_differences(B - 1, 0)
                chunk_lo(B - 1, 0, 0)
                chunk_differences(B - 1, 1, x1t_more)
                with pool.Fori(0, HALF // 2 - 1) as i:
                    chunk_lo(B - 1, 2 * i + 1, 1, x1t_more)
                    chunk_differences(B - 1, 2 * i + 2, x1t)
                    chunk_lo(B - 1, 2 * i + 2, 0, x1t)
                    chunk_differences(B - 1, 2 * i + 3, x1t_more)
                chunk_lo(B - 1, HALF - 1, 1, x1t_more)

            for k in range(4):
                ahead(Half(0, 0, False, True), k)
            batches(pool, half, last)

        @block.scalar
        def _(act):
            A = nc.scalar
            act.wait_ge(S["setup_v"], 1)
            A.activation(grid[:, 0, :], grid[:, 1, :], ACT.Sin).then_inc(S["setup_a"], 1)
            act.wait_ge(S["setup_v"], 2)
            A.activation(grid[:, 1, :], grid[:, 1, :], ACT.Sin).then_inc(S["setup_a"], 1)

            act.wait_ge(S["parts_done"], 1)
            for j in range(2):
                part, hi, lo = gcol_part(j)
                ins = A.copy(hi, part)
            ins.then_inc(S["gcol_hi"], 1)
            act.wait_ge(S["gcol_lo"], 1)
            for j in range(2):
                _, hi, lo = gcol_part(j)
                for im, to in zip((hi[:, 1, :], lo[:, 1, :]), minus_im(j)):
                    ins = A.activation(to, im, ACT.Copy, scale=-1.0)
            ins.then_inc(S["gcol_ready"], 1)

            def root_of_variance1(b):
                act.wait_ge(S["st1_v"], b * 3 + 3)
                A.activation(gn1[:, 3, :], gn1[:, 1, :], ACT.Sqrt).then_inc(S["st1_a"], 1)

            def root_of_variance2(cb):
                act.wait_ge(S["gn2_v"], cb * 4 + 3)
                A.activation(gn2[:, 5:6], gn2[:, 4:5], ACT.Sqrt).then_inc(S["gn2_a"], 1)

            def pair_hi(hf, g, k):
                wait(act, "raw_n", hf.pairs + g + 1)
                A.copy(split[:, k, 0], fold[:, k % 2]).then_inc(S["raw_hi"], 1)

            def normalise(hf, g, k):
                act.wait_ge(S["link1"], (hf.b + 1) * LINKS1)
                act.wait_ge(raw_in[k], (hf.pairs + g) * 8 + (16 - 8 * k))
                A.activation(raw[:, k, 1], raw[:, k, 1], ACT.Identity, bias=gn1[:, 5, bass.ds(g, 1)],
                             scale=gn1[:, 4, bass.ds(g, 1)]).then_inc(S["norm_done"], 1)

            def chunk_hi(cb, e, k, buf=x1t):
                act.wait_ge(S["xc_dif"], cb * HALF + e + 1)
                A.copy(conv_in[:, k, 0], buf[:, :, :]).then_inc(S["xc_hi"], 1)

            def rows_out(cb, c, k):
                act.wait_ge(S["cv_mm"], cb * (3 * HALF) + 3 * c + (2 * k + 1))
                wait(act, f"cv_out{k}", cb * (HALF * 64) + c * 64)
                A.activation(outs[:, k, :, :], psum[:, 5 + 2 * k, :].rearrange("p (j w) -> p j w", j=2),
                             ACT.Identity, bias=gn2[:, 8:9], scale=gn2[:, 9:10]).then_inc(S["cv_part"], 1)

            def ahead(hf, k):
                if hf and k == 0:
                    normalise(hf, 0, 0)
                    normalise(hf, 1, 1)
                    pair_hi(hf, 0, 0)
                if hf and k == 1:
                    pair_hi(hf, 1, 1)
                if hf and k == 2:
                    normalise(hf, 2, 0)

            def half(hf):
                def product_hi(c, s):
                    act.wait_ge(S["s1_mm"], hf.chans + c + 1)
                    A.activation(Z[:, 0, :, 0:hf.rows, bass.ds(c, 1)].rearrange("p k r c -> p k (r c)"),
                                 rows_of(s, hf.rows), ACT.Copy, scale=1.0 / G_SCALE).then_inc(S["z_hi"], 1)

                def pair(g, k):
                    for e in range(2):
                        product_hi(2 * g + e, (2 * k + e) % 4)
                    pair_hi(hf, g + AHEAD, (k + AHEAD) % 4)
                    if not isinstance(g, int) or g + AHEAD + 1 < NPAIR:
                        normalise(hf, g + (AHEAD + 1), (k + AHEAD + 1) % 2)

                pair_hi(hf, 2, 2)
                normalise(hf, 3, 1)
                turns = 1 if hf.h == 0 and hf.conv else 0
                for k in range(4 * turns):
                    pair(k, k)
                if turns:
                    root_of_variance2(hf.b - 1)
                with act.Fori(turns, NPAIR // 4 - 1) as i:
                    for k in range(4):
                        pair(4 * i + k, k)
                pair(NPAIR - 4, 0)
                if hf.h == 0 and hf.conv:
                    chunk_hi(hf.b - 1, 0, 0)
                for c in range(C - 2 * AHEAD, C):
                    product_hi(c, c % 4)

                def angle(u, s):
                    if hf.has(u - 2):
                        v, t, m = u - 2, (s + 2) % 4, hf.blocks(u - 2)
                        act.wait_ge(S["u_done"], hf.first + v + 1)
                        A.activation(ang[:, t, 0:m], ang[:, t, 0:m], ACT.Arctan).then_inc(S["at_done"], 1)
                        A.activation(trf[:, t, 0:m, 1, :], trf[:, t, 0:m, 1, :], ACT.Sign).then_inc(S["sgn_done"], 1)

                def roots(u, s):
                    if hf.has(u):
                        n = hf.blocks(u)
                        wait(act, "y_free", hf.first + u + 1)
                        A.activation(sq[:, s % 2, 0, 0:n], trf[:, s, 0:n, 0, :], ACT.Square)
                        A.activation(sq[:, s % 2, 1, 0:n], trf[:, s, 0:n, 1, :], ACT.Square).then_inc(S["sq_done"], 1)
                        act.wait_ge(S["sum_done"], hf.first + u + 1)
                        A.activation(mag[:, s, 0:n], sq[:, s % 2, 0, 0:n], ACT.Sqrt, bias=tiny[:, 0:1])
                        A.activation(sq[:, s % 2, 1, 0:n], trf[:, s, 0:n, 1, :], ACT.Abs).then_inc(S["r_done"], 1)

                def step(u, s, pair):
                    c = hf.ended(u, pair)
                    if c is not None:
                        rows_out(hf.b - 1, c, 1)
                    if hf.has(u):
                        n = hf.blocks(u)
                        act.wait_ge(S["s2_mm"], hf.first + u + 1)
                        k = 2 * (s % 2)
                        A.copy(odd[:, s % 2, 0:n, :], psum[:, k:k + n, 2 * EW:512])
                        A.copy(trf[:, s, 0:n, :, 0:EW:EW - 1], psum[:, k:k + n, 0:2 * EW]
                               .rearrange("p j (i w) -> p j i w", i=2)[:, :, :, 0:EW:EW - 1]).then_inc(S["odd_done"], 1)
                    angle(u, s)
                    e = hf.next_chunk(pair, 1)
                    if e is not None:
                        chunk_hi(hf.b - 1, e, 1 - pair.k)
                    roots(u, s)
                    if pair is not None and hf.conv and pair.j:
                        rows_out(hf.b - 1, pair.c + HALF // 2 * hf.h, 0)

                def start(k):
                    if k == 2 and hf.h == 1 and hf.stats:
                        root_of_variance1(hf.b + 1)

                walk(act, step, hf.n, start, lambda k: ahead(after(hf), k))

            def last():
                root_of_variance2(B - 1)
                chunk_hi(B - 1, 0, 0)
                with act.Fori(0, HALF // 2 - 1) as i:
                    for k in range(2):
                        chunk_hi(B - 1, 2 * i + (k + 1), 1 - k, (x1t_more, x1t)[k])
                        for e in range(2):
                            rows_out(B - 1, 2 * i + k, e)
                chunk_hi(B - 1, HALF - 1, 1, x1t_more)
                for k in range(4):
                    rows_out(B - 1, HALF - 2 + k // 2, k % 2)

            root_of_variance1(0)
            for k in range(4):
                ahead(Half(0, 0, False, True), k)
            batches(act, half, last)

        @block.vector
        def _(dve):
            V = nc.vector
            chain = [0]

            def link(ins):
                chain[0] += 1
                ins.then_inc(S["link"], 1)
                dve.wait_ge(S["link"], chain[0])

            def first_stats(groups):
                for g in groups:
                    dve.wait_ge(first_in[g % 2], 16 * (g // 2) + 16)
                    for c in range(4):
                        V.bn_stats(bst1[:, 4 * g + c, :], four_channels(g % 2)[:, c, :]).then_inc(S["st1_done"], 1)

            V.memset(ones[:, :], 1.0 / P)
            V.memset(tiny[:, :], 2.0 ** -60)
            dve.wait_ge(S["consts_in"], 16 * 7)
            a = sc[:, 1:2]
            link(V.tensor_scalar(a, sc[:, 0:1], float(np.float32(1e-4)), float(np.float32(2.0 - 1e-4)), ALU.max, ALU.min))
            y, z, acc = ang_s[:, 0, :], ang_s[:, 1, :], ang_s[:, 2, :]
            link(V.tensor_scalar(sc[:, 2:3], a, PI, None, ALU.mult))
            link(V.tensor_scalar(y[:, 0:1], sc[:, 2:3], 0.5, None, ALU.mult))
            link(V.tensor_scalar(y[:, 1:2], sc[:, 2:3], 0.25, None, ALU.mult))
            link(V.tensor_scalar(y[:, 2:3], y[:, 1:2], -1.0, HALF_PI, ALU.mult, ALU.add))
            link(V.tensor_scalar(y[:, 2:3], y[:, 2:3], HALF_PI_LOW, None, ALU.add))
            link(V.tensor_scalar(sc[:, 3:4], y[:, 0:1], -1.0, PI, ALU.mult, ALU.add))
            link(V.tensor_scalar(sc[:, 3:4], sc[:, 3:4], PI_LOW, None, ALU.add))
            link(V.tensor_tensor(y[:, 0:1], y[:, 0:1], sc[:, 3:4], ALU.min))
            link(V.tensor_tensor(z, y, y, ALU.mult))
            fact = [-1 / 6, 1 / 120, -1 / 5040, 1 / 362880, -1 / 39916800, 1 / 6227020800, -1 / 1307674368000]
            link(V.tensor_scalar(acc, z, fact[6], fact[5], ALU.mult, ALU.add))
            for f in fact[4::-1]:
                link(V.tensor_tensor(acc, acc, z, ALU.mult))
                link(V.tensor_scalar(acc, acc, f, None, ALU.add))
            link(V.tensor_tensor(acc, acc, z, ALU.mult))
            link(V.tensor_tensor(acc, acc, y, ALU.mult))
            link(V.tensor_tensor(acc, acc, y, ALU.add))
            link(V.reciprocal(sc[:, 4:5], acc[:, 2:3]))
            link(V.tensor_tensor(sc[:, 5:6], acc[:, 1:2], sc[:, 4:5], ALU.mult))
            link(V.tensor_scalar(sc[:, 6:7], acc[:, 0:1], float(W), None, ALU.mult))
            link(V.reciprocal(sc[:, 7:8], sc[:, 6:7]))
            link(V.tensor_scalar(sc[:, 8:9], acc[:, 0:1], 1e-12, None, ALU.add))
            link(V.reciprocal(sc[:, 9:10], sc[:, 8:9]))
            link(V.tensor_scalar(mixw[:, 0, :], mixw[:, 0, :], sc[:, 9:10], 1.0 / (X_SCALE * G_SCALE), ALU.mult, ALU.mult))
            link(V.tensor_scalar(mixw[:, 1, :], mixw[:, 1, :], -2.0 / float(np.pi), None, ALU.mult))
            th, kk = grid[:, 0, :], grid[:, 1, :]
            link(V.tensor_scalar(th, th, PI, None, ALU.mult))
            link(V.tensor_scalar(th[:, 0:2], th[:, 0:2], sc[:, 5:6], 1.0 / W, ALU.mult, ALU.mult))
            link(V.tensor_scalar(th[:, 4:260], th[:, 4:260], sc[:, 5:6], 1.0 / W, ALU.mult, ALU.mult))
            link(V.tensor_scalar(th[:, 2:4], th[:, 2:4], sc[:, 7:8], None, ALU.mult))
            link(V.tensor_scalar(kk, th, float(1 / (2 * np.pi)), ROUND, ALU.mult, ALU.add))
            link(V.tensor_scalar(kk, kk, ROUND, None, ALU.subtract))
            for part in (TWO_PI_A, TWO_PI_B, TWO_PI_C):
                link(V.scalar_tensor_tensor(th, kk, -part, th, ALU.mult, ALU.add))
            V.tensor_scalar(kk, th, 3.1415925, -3.1415925, ALU.min, ALU.max).then_inc(S["setup_v"], 1)
            dve.wait_ge(S["setup_a"], 1)
            dve.wait_ge(S["setup_v"], 1)
            link(V.scalar_tensor_tensor(kk, kk, -1.0, kk, ALU.mult, ALU.max))
            V.tensor_scalar(kk, kk, -1.0, HALF_PI, ALU.mult, ALU.add).then_inc(S["setup_v"], 1)
            dve.wait_ge(S["setup_a"], 2)
            sin_, cos_ = th, kk
            link(V.tensor_scalar(sc[:, 10:12], sin_[:, 2:4], -1.0, None, ALU.mult))
            for t in range(2):
                for k in range(2):
                    V.tensor_scalar(kern[:, t, k, 0:256], dft[:, t, k, :], cos_[:, 2 + k:3 + k], None, ALU.mult)
                    ins = V.tensor_scalar(kern[:, t, k, 256:512], dft[:, t, k, :], sc[:, 10 + k:11 + k], None, ALU.mult)
            ins.then_inc(S["g_ready"], 1)
            link(V.tensor_scalar(sc[:, 12:14], cos_[:, 0:2], G_SCALE / W, None, ALU.mult))
            link(V.tensor_scalar(sc[:, 14:16], sin_[:, 0:2], G_SCALE / W, None, ALU.mult))
            first_stats(range(0, 3))
            dve.wait_ge(S["w_in"], 16)
            V.tensor_reduce(wmax[:, 2:3], convw_raw[:, 0:2], mybir.AxisListType.XYZ, ALU.min)
            link(V.tensor_reduce(wmax[:, 0:1], convw_raw[:, 0:2], mybir.AxisListType.XYZ, ALU.max))
            V.scalar_tensor_tensor(wmax[:, 0:1], wmax[:, 2:3], -1.0, wmax[:, 0:1], ALU.mult, ALU.max)
            dve.wait_ge(S["setup_mm"], 1)
            rc, rs = cos_[:, 4:260], sin_[:, 4:260]
            work = [[part_tmp[:, 4 * j + n, :] for n in range(4)] + [parts[:, j, 0:256], parts[:, j, 256:512]]
                    for j in range(3)]
            for j, (t0, t1, ur, ui, gr, gi) in enumerate(work):
                V.tensor_scalar(t0, psum[:, j, 0:256], sc[:, 12 + j // 2:13 + j // 2], None, ALU.mult)
                ins = V.tensor_scalar(t1, psum[:, j, 0:256], sc[:, 14 + j // 2:15 + j // 2], None, ALU.mult)
            link(ins)
            for j, (t0, t1, ur, ui, gr, gi) in enumerate(work):
                V.scalar_tensor_tensor(ur, psum[:, j, 256:512], sc[:, 14 + j // 2:15 + j // 2], t0, ALU.mult, ALU.add)
                ins = V.scalar_tensor_tensor(ui, psum[:, j, 256:512], sc[:, 12 + j // 2:13 + j // 2], t1,
                                             ALU.mult, ALU.subtract)
            link(ins)
            for t0, t1, ur, ui, gr, gi in work:
                V.tensor_tensor(gr, ur, rc, ALU.mult)
                V.tensor_tensor(t1, ui, rs, ALU.mult)
                V.tensor_tensor(gi, ui, rc, ALU.mult)
                ins = V.tensor_tensor(t0, ur, rs, ALU.mult)
            link(ins)
            for t0, t1, ur, ui, gr, gi in work:
                V.tensor_tensor(gr, gr, t1, ALU.add)
                ins = V.tensor_tensor(gi, gi, t0, ALU.subtract)
            ins.then_inc(S["parts_done"], 1)
            dve.wait_ge(S["parts_done"], 1)
            link(V.tensor_tensor(g_sum, parts[:, 0, :], parts[:, 1, :], ALU.add))
            rows = [full.rearrange("p (i n) -> p i n", i=2) for full in (g_sum, parts[:, 2, :])]
            for j in range(2):
                ins = V.tensor_copy(Grow[:, 0, j, :, 1:1 + H], rows[j])
            link(ins)
            for j in range(2):
                ins = V.tensor_tensor(Grow[:, 1, j, :, 1:1 + H], rows[j], Grow[:, 0, j, :, 1:1 + H], ALU.subtract)
            link(ins)
            for to, of in ((0, 2), (H + 1, H - 1), (H + 2, H - 2), (H + 3, 3)):
                for t in range(2):
                    V.tensor_copy(Grow[:, t, :, :, to:to + 1], Grow[:, t, :, :, of:of + 1])
            V.tensor_scalar(neg_mid[0:1, :, :], Grow[0:1, :, 1, 1, 1:1 + EW], -1.0, None, ALU.mult)\
                .then_inc(S["g_ready"], 1)
            first_stats(range(3, C // 4))

            def pair_stats(b, p):
                for k in range(2):
                    dve.wait_ge(st_in[k], (b - 1) * (16 * NPAIR) + 16 * p + 16)
                    V.bn_stats(bst1[:, bass.ds(2 * p + k, 1), :].rearrange("p c s -> p (c s)"), stat_in[:, k, :])\
                        .then_inc(S["st1_done"], 1)

            def link1(ins, b, n):
                ins.then_inc(S["link1"], 1)
                dve.wait_ge(S["link1"], b * LINKS1 + n)

            mean, var, w0, w1 = (gn1[:, n, :] for n in range(4))

            def spread1(b):
                dve.wait_ge(S["st1_done"], (b + 1) * C + PRIME["st1_done"])
                V.memset(gn1[:, 2:4, :], 0.0)
                for g in range(NPAIR):
                    ins = V.bn_aggr(mv1[:, g, :], bst1[:, 2 * g:2 * g + 2, :].rearrange("p c s -> p (c s)"))
                ins.then_inc(S["st1_v"], 1)

            def mean1(b):
                dve.wait_ge(S["st1_p"], b * 2 + 1)
                link1(V.tensor_copy(gn1[:, 0:2, :], sums1.rearrange("p (g s) -> p s g", s=2)), b, 1)
                link1(V.tensor_tensor(w0, mv1[:, :, 0], mean, ALU.subtract), b, 2)
                V.tensor_tensor(w0, w0, w0, ALU.mult).then_inc(S["st1_v"], 1)

            def scale1(b):
                dve.wait_ge(S["st1_p"], b * 2 + 2)
                dve.wait_ge(S["st1_v"], b * 3 + 2)
                V.scalar_tensor_tensor(var, sums1_sq, EPS, var, ALU.add, ALU.add)\
                    .then_inc(S["st1_v"], 1)
                dve.wait_ge(S["st1_a"], b + 1)
                dve.wait_ge(S["st1_v"], b * 3 + 3)
                link1(V.reciprocal(w0, w1), b, 3)
                link1(V.tensor_tensor(w0, w0, var, ALU.mult), b, 4)
                link1(V.tensor_tensor(w0, w0, w1, ALU.add), b, 5)
                link1(V.tensor_scalar(w0, w0, 0.5, None, ALU.mult), b, 6)
                link1(V.reciprocal(w0, w0), b, 7)
                link1(V.tensor_scalar(gn1[:, 4, :], w0, X_SCALE, None, ALU.mult), b, 8)
                link1(V.tensor_tensor(w0, mean, gn1[:, 4, :], ALU.mult), b, 9)
                V.tensor_scalar(gn1[:, 5, :], w0, -1.0, None, ALU.mult).then_inc(S["link1"], 1)

            spread1(0)
            mean1(0)
            scale1(0)

            def link2(ins, b, n):
                ins.then_inc(S["link2"], 1)
                dve.wait_ge(S["link2"], b * LINKS2 + n)

            def fold_pair(hf, g, k):
                dve.wait_ge(S["link1"], (hf.b + 1) * LINKS1)
                dve.wait_ge(raw_in[k], (hf.pairs + g) * 8 + (16 - 8 * k))
                V.tensor_scalar(raw[:, k, 0], raw[:, k, 0], gn1[:, 4, bass.ds(g, 1)], gn1[:, 5, bass.ds(g, 1)],
                                ALU.mult, ALU.add).then_inc(S["norm_own"], 1)
                wait(dve, "raw_lo", hf.pairs + g - 1)
                for c in range(2):
                    dve.wait_ge(S["norm_done" if c else "norm_own"], hf.pairs + g + 1)
                    a = raw[:, k, c]
                    V.tensor_tensor(fold[:, k, 0, c, :, 1:P], a[:, :, 1:P], a[:, :, W - 1:P:-1], ALU.add)
                    V.tensor_tensor(fold[:, k, 1, c, :, 1:P], a[:, :, 1:P], a[:, :, W - 1:P:-1], ALU.subtract)
                a = raw[:, k].rearrange("p c k w -> p (c k) w")
                e = fold[:, k].rearrange("p f c k w -> p f (c k) w")
                V.tensor_copy(e[:, :, :, 0].rearrange("p f n -> p n f"), a[:, :, 0:P + 1:P]).then_inc(S["raw_n"], 1)

            def ahead(hf, k):
                if hf and k in (0, 1, 3):
                    fold_pair(hf, k - k // 3, (0, 1, None, 0)[k])

            def normalise_x1(cb, e, buf=x1t, loads=None):
                dve.wait_ge(S["xc_in" if buf is x1t else "xc_more_in"], (cb * HALF + e + 1 if loads is None else loads) * 16)
                V.tensor_scalar(buf[:, 0:CB, 1:1 + W], buf[:, 0:CB, 1:1 + W], gn2[:, 11:12], gn2[:, 12:13],
                                ALU.mult, ALU.add).then_inc(S["xc_pad"], 1)
                dve.wait_ge(S["xc_pad"], cb * HALF + e + 1)
                V.tensor_copy(buf[:, 0:CB, 0:1], buf[:, 0:CB, 2:3])
                V.tensor_copy(buf[:, 0:CB, W + 1:W + 2], buf[:, 0:CB, W - 1:W])
                V.tensor_copy(buf[:, 0:CB, W + 2:W + 3], buf[:, 0:CB, W - 2:W - 1])
                V.tensor_copy(buf[:, 0:CB, W + 3:W + 4], buf[:, 0:CB, 3:4]).then_inc(S["xc_n"], 1)

            def add_middle(cb, c):
                dve.wait_ge(S["cv_mm"], cb * (3 * HALF) + 3 * c + 2)
                for k in range(2):
                    wait(dve, "cv_part", cb * NOUT + 2 * c + (k + 1))
                    V.scalar_tensor_tensor(outs[:, k], psum[:, 6, :].rearrange("p (j w) -> p j w", j=2), gn2[:, 9:10],
                                           outs[:, k], ALU.mult, ALU.add).then_inc(S["cv_free"], 1)

            def spread2(b):
                dve.wait_ge(S["st2_done"], (b + 1) * NBLK)
                link2(V.tensor_copy(bst2[0:C, 0, :], bst2[0:C, NBLK - 1, :]), b, 1)
                V.memset(gn2[:, 4:8], 0.0)
                V.bn_aggr(gn2[:, 0:2], bst2[:, 0:NBLK - 1, :].rearrange("p j s -> p (j s)")).then_inc(S["gn2_v"], 1)

            def mean2(b):
                dve.wait_ge(S["gn2_p"], b * 3 + 1)
                link2(V.tensor_copy(gn2[:, 2:4], sums2[:, 0:2]), b, 2)
                link2(V.tensor_tensor(gn2[:, 6:7], gn2[:, 0:1], gn2[:, 2:3], ALU.subtract), b, 3)
                V.tensor_tensor(gn2[:, 7:8], gn2[:, 6:7], gn2[:, 6:7], ALU.mult).then_inc(S["gn2_v"], 1)

            def var2(b):
                dve.wait_ge(S["gn2_p"], b * 3 + 2)
                dve.wait_ge(S["gn2_v"], b * 4 + 2)
                V.scalar_tensor_tensor(gn2[:, 4:5], sums2[:, 2:3], EPS, gn2[:, 3:4], ALU.add, ALU.add)\
                    .then_inc(S["gn2_v"], 1)

            def scale2(b):
                dve.wait_ge(S["gn2_a"], b + 1)
                dve.wait_ge(S["gn2_v"], b * 4 + 3)
                link2(V.reciprocal(gn2[:, 6:7], gn2[:, 5:6]), b, 4)
                link2(V.tensor_tensor(gn2[:, 6:7], gn2[:, 6:7], gn2[:, 4:5], ALU.mult), b, 5)
                link2(V.tensor_tensor(gn2[:, 6:7], gn2[:, 6:7], gn2[:, 5:6], ALU.add), b, 6)
                link2(V.tensor_scalar(gn2[:, 10:11], gn2[:, 6:7], 0.5, None, ALU.mult), b, 7)
                V.tensor_tensor(wmax[:, 1:2], wmax[:, 0:1], gn2[:, 10:11], ALU.add).then_inc(S["gn2_v"], 1)
                link2(V.reciprocal(gn2[:, 7:8], gn2[:, 10:11]), b, 8)
                link2(V.tensor_scalar(gn2[:, 11:12], gn2[:, 7:8], X_SCALE, None, ALU.mult), b, 9)
                link2(V.scalar_tensor_tensor(gn2[:, 12:13], gn2[:, 2:3], -1.0, gn2[:, 11:12], ALU.mult, ALU.mult), b, 10)
                dve.wait_ge(S["w_in"], (b + 2) * 16)
                V.scalar_tensor_tensor(convw_raw[:, 0:2, 3, :], tapm[:, :, :], gn2[:, 10:11], convw_raw[:, 0:2, 3, :],
                                       ALU.mult, ALU.add).then_inc(S["link2"], 1)

            def factor2(b):
                dve.wait_ge(S["gn2_p"], b * 3 + 3)
                link2(V.tensor_scalar(gn2[:, 13:14].bitcast(I32), sums2[:, 3:4].bitcast(I32), 0x7F800000, None,
                                      ALU.bitwise_and), b, 12)
                V.tensor_copy(gn2[:, 8:9], gn2[:, 2:3])
                V.tensor_scalar(gn2[:, 9:10], gn2[:, 13:14], 1.0 / (W_SCALE * X_SCALE), None, ALU.mult)
                link2(V.reciprocal(gn2[:, 14:15], gn2[:, 13:14]), b, 13)
                link2(V.tensor_tensor(convw_raw[:, 2], convw_raw[:, 0], convw_raw[:, 1], ALU.add), b, 14)
                V.tensor_scalar(gn2[:, 14:15], gn2[:, 14:15], W_SCALE, None, ALU.mult).then_inc(S["link2"], 1)

            def weights(b):
                dve.wait_ge(S["link2"], (b + 1) * LINKS2)
                V.tensor_scalar(convw[:, 0], convw_raw[:, :, :, :], gn2[:, 14:15], None, ALU.mult)\
                    .then_inc(S["w_ready"], 1)
                wait(dve, "w_ready", b * 2 + 1)
                V.scalar_tensor_tensor(convw[:, 1], convw_raw[:, :, :, :], gn2[:, 14:15], convw[:, 0],
                                       ALU.mult, ALU.subtract).then_inc(S["w_ready"], 1)

            def half(hf):
                b = hf.b

                def product_lo(c, s):
                    dve.wait_ge(S["z_hi"], hf.chans + c + 1)
                    V.scalar_tensor_tensor(Z[:, 1, :, 0:hf.rows, bass.ds(c, 1)].rearrange("p k r c -> p k (r c)"),
                                           rows_of(s, hf.rows), 1.0 / G_SCALE,
                                           Z[:, 0, :, 0:hf.rows, bass.ds(c, 1)].rearrange("p k r c -> p k (r c)"),
                                           ALU.mult, ALU.subtract).then_inc(S["s1_free"], 1)

                def pair(g, k):
                    fold_pair(hf, g + AHEAD, (k + AHEAD) % 2)
                    for e in range(2):
                        product_lo(2 * g + e, (2 * k + e) % 4)

                parts = {1: mean2, 3: var2, 4: scale2, 5: factor2} if hf.h == 0 and hf.conv else {}
                if parts:
                    spread2(b - 1)
                peeled = 7 if parts else 1
                for g in range(peeled):
                    pair(g, g)
                    if g in parts:
                        parts[g](b - 1)
                with dve.Fori(0, (NPAIR - AHEAD - peeled) // 2) as i:
                    for k in range(2):
                        pair(2 * i + (k + peeled), k + peeled)
                if parts:
                    normalise_x1(b - 1, 0)
                    weights(b - 1)
                for c in range(C - 2 * AHEAD, C):
                    product_lo(c, c % 4)

                def step(u, s, pair):
                    c = hf.ended(u, pair)
                    if c is not None:
                        add_middle(b - 1, c)
                    if hf.has(u):
                        n, k = hf.blocks(u), 2 * (s % 2)
                        dve.wait_ge(S["odd_done"], hf.first + u + 1)
                        ev = psum[:, k:k + n, 0:2 * EW].rearrange("p j (i w) -> p j i w", i=2)[:, :, :, 1:EW - 1]
                        od = odd[:, s % 2, 0:n, :].rearrange("p j (i w) -> p j i w", i=2)
                        V.tensor_tensor(trf[:, s, 0:n, :, 1:EW - 1], ev, od, ALU.add)
                        V.tensor_tensor(trf[:, s, 0:n, :, W - 1:EW - 1:-1], ev, od, ALU.subtract).then_inc(S["y_free"], 1)
                    if hf.has(u - 1):
                        v, t, m = u - 1, (s + 3) % 4, hf.blocks(u - 1)
                        d = sq[:, t % 2, 0, 0:m]
                        dve.wait_ge(S["d_done"], hf.first + v + 1)
                        V.reciprocal(d, d).then_inc(S["rec_done"], 1)
                    if hf.has(u - 2):
                        v, t, m = u - 2, (s + 2) % 4, hf.blocks(u - 2)
                        dve.wait_ge(S["sgn_done"], hf.first + v + 1)
                        V.scalar_tensor_tensor(ang[:, t, 0:m], ang[:, t, 0:m], float(np.pi / 4), trf[:, t, 0:m, 1, :],
                                               ALU.subtract, ALU.mult).then_inc(S["ang_done"], 1)
                    if hf.has(u - 3):
                        v, t, m = u - 3, (s + 1) % 4, hf.blocks(u - 3)
                        per = 9 if t == 0 else 8
                        dve.wait_ge(S["mix_mm"], hf.first + v + 1)
                        if isinstance(v, int):
                            dve.wait_ge(res_in[t], b * (64 * per) + 256 * hf.h + 64 * (v // 4 + 1))
                        else:
                            dve.wait_ge(res_in[t], b * (64 * per) + 256 * hf.h + 16 * v + (64 - 16 * t))
                        V.tensor_tensor(res[:, t, 0:m, :], psum[:, 4, 0:256 * m].rearrange("p (j w) -> p j w", j=m),
                                        res[:, t, 0:m, :], ALU.add).then_inc(S["x1_done"], 1)
                        dve.wait_ge(S["x1_done"], hf.first + v + 1)
                        for e in range(m):
                            V.bn_stats(bst2[:, bass.ds(2 * v + (e + 2 * HALF * hf.h), 1), :].rearrange("p c s -> p (c s)"),
                                       res[:, t, e, :]).then_inc(S["st2_done"], 1)
                    if hf.stat(u) is not None:
                        pair_stats(b + 1, u - 3)
                    e = hf.next_chunk(pair, 0)
                    if e is not None:
                        normalise_x1(b - 1, e)

                def start(k):
                    if hf.h == 1 and hf.stats:
                        (spread1, mean1, scale1)[k](b + 1)

                walk(dve, step, hf.n, start, lambda k: ahead(after(hf), k))

            def last():
                for part in (spread2, mean2, var2, scale2, factor2):
                    part(B - 1)
                normalise_x1(B - 1, 0)
                weights(B - 1)
                normalise_x1(B - 1, 1, x1t_more, 1)
                with dve.Fori(0, HALF // 2 - 1) as i:
                    for e, buf, loads in ((0, x1t, (B - 1) * HALF + i + 2), (1, x1t_more, i + 2)):
                        normalise_x1(B - 1, 2 * i + (e + 2), buf, loads)
                        add_middle(B - 1, 2 * i + e)
                for c in (HALF - 2, HALF - 1):
                    add_middle(B - 1, c)

            for k in range(4):
                ahead(Half(0, 0, False, True), k)
            batches(dve, half, last)

        @block.tensor
        def _(pe):
            T = nc.tensor
            pe.wait_ge(S["g_ready"], 1)
            for j, r, tables in ((0, 0, (0,)), (1, 0, (1,)), (2, 1, (0, 1))):
                terms = [(t, k) for t in tables for k in range(2)]
                for t, k in terms:
                    ins = T.matmul(psum[:, j, :], dft[:, t, k, P * r:P * r + P], kern[:, t, k, :],
                                   start=(t, k) == terms[0], stop=(t, k) == terms[-1])
            ins.then_inc(S["setup_mm"], 1)

            def sum1(b, n):
                pe.wait_ge(S["st1_v"], b * 3 + (n + 1))
                if n == 0:
                    T.matmul(sums1, ones[:, :], mv1[:, :, :].rearrange("p g s -> p (g s)"), start=True, stop=True)\
                        .then_inc(S["st1_p"], 1)
                else:
                    T.matmul(sums1_sq, ones[:, :], gn1[:, 2, :], start=True, stop=True).then_inc(S["st1_p"], 1)

            def sum2(cb, n):
                pe.wait_ge(S["gn2_v"], cb * 4 + (1, 2, 4)[n])
                to, by, of = ((sums2[:, 0:2], quadm, gn2[:, 0:2]), (sums2[:, 2:3], quadm, gn2[:, 7:8]),
                              (sums2[:, 3:4], ones, wmax[:, 1:2]))[n]
                T.matmul(to, by[:, :], of, start=True, stop=True).then_inc(S["gn2_p"], 1)

            def sum2_read(cb, n):
                name, value = (("link2", cb * LINKS2 + 2), ("gn2_v", cb * 4 + 3), ("link2", cb * LINKS2 + 12))[n]
                pe.wait_ge(S[name], value)

            def conv_part(cb, chunk, k, j):
                wait(pe, "w_ready", cb * 2 + 2)
                wait(pe, "xc_lo", cb * HALF + chunk + 1)
                passes = [(kx, xt, wt) for kx in range(KT) for xt, wt in ((0, 0), (1, 0), (0, 1))]
                cut = len(passes) // 2
                for n, mine in ((0, passes), (1, passes[:cut])) if j == 0 else ((1, passes[cut:]), (2, passes)):
                    if n == 0:
                        wait(pe, "cv_part", cb * NOUT + 2 * chunk - 1)
                    if n == 1 and j == 0:
                        wait(pe, "cv_free", cb * NOUT + 2 * chunk)
                    if n == 2:
                        wait(pe, "cv_part", cb * NOUT + 2 * chunk)
                    blocks = (slice(0, 6, 5), slice(1, 4, 2), slice(2, 5, 2))[n]
                    for kx, xt, wt in mine:
                        ins = T.matmul(psum[:, 5 + n, :], convw[:, wt, (0, 2, 1)[n], kx, :],
                                       conv_in[:, k, xt, blocks, 4 - kx:4 - kx + W],
                                       start=(kx, xt, wt) == passes[0], stop=(kx, xt, wt) == passes[-1])
                    if n != 1 or j == 1:
                        ins.then_inc(S["cv_mm"], 1)

            def half(hf):
                b, R = hf.b, hf.rows
                first_row = ROWS[0] * hf.h

                def channel(c, k, e, sums=None):
                    s = (2 * k + e) % 4
                    wait(pe, "s1_free", hf.chans + c - 3)
                    first = not isinstance(hf.first, int) or hf.first > 0
                    if first and s == 0:
                        wait(pe, "y_free", hf.first)
                    if first and s == 2:
                        pe.wait_ge(S["x1_done"], hf.first)
                    if s >= 2 and hf.conv:
                        wait(pe, "cv_free", (b - 1) * NOUT + HALF * hf.h)
                    if sums is not None:
                        sum2(b - 1, sums)
                    for f in range(2):
                        n = 0
                        if f == 1 and sums is not None:
                            sum2_read(b - 1, sums)
                        for kb in range(NB):
                            for xt, gt in ((0, 0), (0, 1), (1, 0)):
                                ins = T.matmul(psum[:, 2 * s + f, :].rearrange("p (i r) -> p i r", i=2)[:, :, 0:R],
                                               split[:, k, xt, f, e, kb, :],
                                               Grow[:, gt, kb, :, first_row:first_row + R], start=n == 0, stop=n == 5)
                                n += 1
                    ins.then_inc(S["s1_mm"], 1)

                pe.wait_ge(S["g_ready"], 2)
                def rows_pair(g, k, sums=None):
                    wait(pe, "raw_lo", hf.pairs + g + 1)
                    for e in range(2):
                        channel(2 * g + e, k, e, None if e else sums)

                turns = 2 if hf.h == 0 and hf.conv else 0
                for g in range(4 * turns):
                    rows_pair(g, g % 4, {3: 0, 5: 1, 7: 2}.get(g))
                with pe.Fori(turns, NPAIR // 4) as i:
                    for k in range(4):
                        rows_pair(4 * i + k, k)

                def transform(u, s, n):
                    if isinstance(u, int) and u == 0:
                        pe.wait_ge(S["gcol_ready"], 1)
                        pe.wait_ge(S["mid_in"], 192)
                        pe.wait_ge(S["zmid_in"], (b * 2 + hf.h + 1) * 96)
                    wait(pe, "y_free", hf.first + u - 1)
                    for j in range(n):
                        cols = bass.ds((2 * u + j) * P, P)
                        for f, base, w, at in ((0, 0, EW, 0), (1, 3 * EW, OW, 2 * EW)):
                            dst = psum[:, 2 * (s % 2) + j, at:at + 2 * w]
                            m = 0
                            for ri in range(2):
                                for zt, gt in ((0, 0), (0, 1), (1, 0)):
                                    c0 = base + (1 - ri) * w
                                    ins = T.matmul(dst, Zflat[:, 4 * zt + 2 * f + ri, cols], Gcol[:, gt, c0:c0 + 2 * w],
                                                   start=m == 0, stop=f == 1 and m == 5)
                                    m += 1
                            if f == 0:
                                ins = T.matmul(dst, Zmid[:, cols], Gmid[:, :], start=False, stop=True)
                    ins.then_inc(S["s2_mm"], 1)

                def mix(u, s, n):
                    pe.wait_ge(S["ang_done"], hf.first + u + 1)
                    if not isinstance(hf.first + u, int) or hf.first + u > 0:
                        pe.wait_ge(S["x1_done"], hf.first + u)
                    dst = psum[:, 4, 0:256 * n]
                    T.matmul(dst, mixw[:, 0, :], mag[:, s, 0:n].rearrange("p j w -> p (j w)"), start=True, stop=False)
                    T.matmul(dst, mixw[:, 1, :], ang[:, s, 0:n].rearrange("p j w -> p (j w)"),
                             start=False, stop=True).then_inc(S["mix_mm"], 1)

                def step(u, s, pair):
                    if isinstance(u, int) and u == 0:
                        wait(pe, "s1_free", hf.chans + C)
                    def part():
                        if pair is not None and hf.conv:
                            conv_part(b - 1, pair.c + HALF // 2 * hf.h, pair.k, pair.j)

                    early = isinstance(u, int) and u in (0, HALF + 1)
                    if early:
                        part()
                    if hf.has(u):
                        transform(u, s, hf.blocks(u))
                    if hf.has(u - 3):
                        mix(u - 3, (s + 1) % 4, hf.blocks(u - 3))
                    if not early:
                        part()

                def start(k):
                    if k and hf.h == 1 and hf.stats:
                        sum1(b + 1, k - 1)

                walk(pe, step, hf.n, start, lambda k: None)

            def last():
                wait(pe, "cv_free", (B - 1) * NOUT)
                for n in range(3):
                    sum2(B - 1, n)
                with pe.Fori(0, HALF // 2) as i:
                    for k in range(2):
                        for j in range(2):
                            conv_part(B - 1, 2 * i + k, k, j)

            for n in range(2):
                sum1(0, n)
            batches(pe, half, last)


def kernel(**inputs):
    import concourse.bacc as bacc
    from concourse.bass_utils import run_bass_kernel_spmd

    f32 = mybir.dt.float32
    x = np.ascontiguousarray(inputs["x"])
    B, C, H, W = x.shape
    Q = P // C
    w0 = np.asarray(inputs["L0_conv_w"])
    w1 = np.asarray(inputs["L1_conv_weight"])
    KT = w1.shape[-1]

    mix_w = np.zeros((P, 2, P), w0.dtype)
    for q in range(Q):
        for part in range(2):
            mix_w[q * C:(q + 1) * C, part, q * C:(q + 1) * C] = w0[:, part * C:(part + 1) * C].T
    conv_w = np.zeros((P, 2, KT, P), w1.dtype)
    tap = np.zeros((P, 2, P), np.float32)
    for q in range(Q):
        for ky in range(KT):
            kb, qi = divmod(q + 4 - ky, Q)
            for kx in range(KT):
                conv_w[qi * C:(qi + 1) * C, kb, kx, q * C:(q + 1) * C] = w1[:, :, ky, kx].T
        kb, qi = divmod(q + 1, Q)
        tap[qi * C:(qi + 1) * C, kb, q * C:(q + 1) * C] = np.eye(C, dtype=np.float32)
    group = (np.arange(P) % C) // 2
    quad_mean = ((group[:, None] == group[None, :]) / (2.0 * Q)).astype(np.float32)
    n = np.arange(W)
    pos = np.minimum(n, W - n).astype(np.float64) ** 2
    frq = (n - W // 2).astype(np.float64) ** 2
    grid_sq = np.concatenate([pos.reshape(2, P).T, frq.reshape(2, P).T, np.tile(pos, (P, 1))], axis=1).astype(np.float32)
    turn = 2 * np.pi * (np.outer(n, n) % W) / W
    arrays = {
        "x": x, "alpha": np.asarray(inputs["L0_conv_alpha"]).reshape(1, 1), "grid_sq": grid_sq,
        "dft_cos": np.cos(turn).astype(np.float32), "dft_sin": np.sin(turn).astype(np.float32),
        "mix_w": mix_w, "conv_w": conv_w, "tap": tap, "quad_mean": quad_mean,
    }
    nc = bacc.Bacc("TRN2", target_bir_lowering=False, num_devices=1)
    args = [nc.dram_tensor(k, a.shape, f32, kind="ExternalInput").ap() for k, a in arrays.items()]
    args.append(nc.dram_tensor("out", x.shape, f32, kind="ExternalOutput").ap())
    args.append(nc.dram_tensor("x1_dram", (B, P, H // Q + 1, W), f32, kind="Internal").ap())
    frft_conv_kernel(nc, *args)
    r = run_bass_kernel_spmd(nc, [arrays], core_ids=[0])
    return r.results[0]["out"]
```
